# Optimizing a Trainium2 kernel written in Bass

```python
import numpy as np
import jax
import jax.numpy as jnp

def _softmax(x, axis=-1):
    return jax.nn.softmax(x, axis=axis)

def _gelu(x):
    return jax.nn.gelu(x, approximate=True)

def _silu(x):
    return jax.nn.silu(x)

def _sigmoid(x):
    return jax.nn.sigmoid(x)

def _layernorm(x, axis=-1, eps=1e-05):
    m = jnp.mean(x, axis=axis, keepdims=True)
    v = jnp.var(x, axis=axis, keepdims=True)
    return (x - m) / jnp.sqrt(v + eps)

def _scatter_add(tgt, idx, src, axis=0):
    return tgt.at[idx].add(src)

def _segment_sum(src, seg, n):
    return jax.ops.segment_sum(src, seg, n)
kernel_name = 'mk_gnn_resnorm_d4_gnn_r16_d1076e'

def setup_inputs(seed: int=0):
    np.random.seed(seed)
    _w = jnp.asarray

    def _rec_inputs():
        import jax
        import jax.numpy as jnp
        _gk = jax.random.key(seed)
        x = -0.0003713 + 1 * jax.random.normal(jax.random.fold_in(_gk, 1), (6250, 128), jnp.float32)
        _s = jax.random.randint(jax.random.fold_in(_gk, 2), (50000,), 0, 6250, jnp.int32)
        _d = jax.random.randint(jax.random.fold_in(_gk, 3), (50000,), 0, 6250, jnp.int32)
        _loop = jnp.arange(6250, dtype=jnp.int32)
        src = jnp.concatenate([_s, _d, _loop])
        dst = jnp.concatenate([_d, _s, _loop])
        _o = jnp.argsort(dst, stable=True)
        src = src[_o]
        dst = dst[_o]
        edge_weight = jax.random.uniform(jax.random.fold_in(_gk, 12), (106250,), jnp.float32, 0.0, 0.999998)
        return (x, src, dst, edge_weight)
    x, src, dst, edge_weight = _rec_inputs()

    def _L0_gnn_setup():
        import jax, jax.numpy as jnp
        import numpy as np
        N = 6250
        E = 100000
        D_IN = 128
        D_HID = 128
        D_OUT = 128

        def _sage_conv(h, src, dst, Wl, bl, Wr):
            msgs = h[src]
            agg = jax.ops.segment_sum(msgs, dst, num_segments=N)
            deg = jax.ops.segment_sum(jnp.ones((src.shape[0],), h.dtype), dst, num_segments=N)
            agg = agg / jnp.maximum(deg, 1.0)[:, None]
            return agg @ Wl.T + bl + h @ Wr.T
        key = jax.random.key(seed)
        ks = jax.random.split(key, 8)
        x = jax.random.normal(ks[0], (N, D_IN), dtype=jnp.float32)
        edge_index = jax.random.randint(ks[1], (2, E), 0, N, dtype=jnp.int64)
        s = 0.02
        W1l = jax.random.normal(ks[2], (D_HID, D_IN), dtype=jnp.float32) * s
        b1l = jnp.zeros((D_HID,), dtype=jnp.float32)
        W1r = jax.random.normal(ks[3], (D_HID, D_IN), dtype=jnp.float32) * s
        W2l = jax.random.normal(ks[4], (D_OUT, D_HID), dtype=jnp.float32) * s
        b2l = jnp.zeros((D_OUT,), dtype=jnp.float32)
        W2r = jax.random.normal(ks[5], (D_OUT, D_HID), dtype=jnp.float32) * s
        return {'x': x, 'edge_index': edge_index, 'W1l': W1l, 'b1l': b1l, 'W1r': W1r, 'W2l': W2l, 'b2l': b2l, 'W2r': W2r}
    _L0_gnn_all = _L0_gnn_setup()
    _L0_gnn_in = {k: v for k, v in _L0_gnn_all.items() if k in ('W1l', 'b1l', 'W1r', 'W2l', 'b2l', 'W2r')}
    del _L0_gnn_all

    def _L1_gnn_setup():
        import jax, jax.numpy as jnp
        import numpy as np
        N_NODES = 6250
        N_EDGES = 100000
        IN_DIM, HID_DIM, OUT_DIM = (128, 64, 128)

        def gcn_conv(x, edge_index, W, b):
            n = x.shape[0]
            loop = jnp.arange(n, dtype=edge_index.dtype)
            src = jnp.concatenate([edge_index[0], loop])
            dst = jnp.concatenate([edge_index[1], loop])
            deg = jax.ops.segment_sum(jnp.ones_like(dst, dtype=x.dtype), dst, num_segments=n)
            dinv = jnp.where(deg > 0, jax.lax.rsqrt(deg), 0.0)
            norm = dinv[src] * dinv[dst]
            h = x @ W
            msg = h[src] * norm[:, None]
            agg = jax.ops.segment_sum(msg, dst, num_segments=n)
            return agg + b
        key = jax.random.key(seed)
        k1, k2, k3, k4 = jax.random.split(key, 4)
        x = jax.random.normal(k1, (N_NODES, IN_DIM), dtype=jnp.float32)
        edge_index = jax.random.randint(k2, (2, N_EDGES), 0, N_NODES, dtype=jnp.int32)
        W_conv = jax.random.normal(k3, (IN_DIM, HID_DIM), dtype=jnp.float32) * (1.0 / np.sqrt(IN_DIM))
        b_conv = jnp.zeros((HID_DIM,), dtype=jnp.float32)
        W_lin = jax.random.normal(k4, (HID_DIM, OUT_DIM), dtype=jnp.float32) * (1.0 / np.sqrt(HID_DIM))
        b_lin = jnp.zeros((OUT_DIM,), dtype=jnp.float32)
        return {'x': x, 'edge_index': edge_index, 'W_conv': W_conv, 'b_conv': b_conv, 'W_lin': W_lin, 'b_lin': b_lin}
    _L1_gnn_all = _L1_gnn_setup()
    _L1_gnn_in = {k: v for k, v in _L1_gnn_all.items() if k in ('W_conv', 'b_conv', 'W_lin', 'b_lin')}
    del _L1_gnn_all

    def _L2_gnn_setup():
        import jax, jax.numpy as jnp
        import numpy as np
        N_NODES = 6250

        def gcn_conv(x, edge_index, W, b):
            n = x.shape[0]
            h = x @ W
            loop = jnp.arange(n, dtype=edge_index.dtype)
            src = jnp.concatenate([edge_index[0], loop])
            dst = jnp.concatenate([edge_index[1], loop])
            deg = jax.ops.segment_sum(jnp.ones_like(dst, dtype=h.dtype), dst, num_segments=n)
            dinv = jnp.where(deg > 0, jax.lax.rsqrt(deg), 0.0)
            norm = dinv[src] * dinv[dst]
            msg = h[src] * norm[:, None]
            out = jax.ops.segment_sum(msg, dst, num_segments=n)
            return out + b
        key = jax.random.key(seed)
        k1, k2, k3, k4 = jax.random.split(key, 4)
        nfeat = nhid = 128
        x = jax.random.normal(k1, (N_NODES, nfeat), dtype=jnp.float32)
        edge_index = jax.random.randint(k2, (2, 40000), 0, N_NODES, dtype=jnp.int64)
        s = 1.0 / np.sqrt(nfeat)
        W1 = jax.random.normal(k3, (nfeat, nhid), dtype=jnp.float32) * s
        W2 = jax.random.normal(k4, (nhid, nhid), dtype=jnp.float32) * s
        b1 = jnp.zeros((nhid,), dtype=jnp.float32)
        b2 = jnp.zeros((nhid,), dtype=jnp.float32)
        return {'x': x, 'edge_index': edge_index, 'W1': W1, 'b1': b1, 'W2': W2, 'b2': b2}
    _L2_gnn_all = _L2_gnn_setup()
    _L2_gnn_in = {k: v for k, v in _L2_gnn_all.items() if k in ('W1', 'b1', 'W2', 'b2')}
    del _L2_gnn_all

    def _L3_gnn_setup():
        import jax, jax.numpy as jnp
        import numpy as np
        LN_EPS = 1e-05
        K = 3
        NUM_LAYERS = 3
        key = jax.random.key(seed)
        ks = jax.random.split(key, 6)
        N, E, D = (3125, 40000, 128)
        node = jax.random.normal(ks[0], (N, D), dtype=jnp.float32)
        edge_index = jax.random.randint(ks[1], (2, E), 0, N, dtype=jnp.int32)
        edge_attr = jax.random.uniform(ks[2], (E,), dtype=jnp.float32)
        batch_ptr = jnp.sort(jax.random.randint(ks[3], (11,), 0, N, dtype=jnp.int32))
        W = jax.random.normal(ks[4], (NUM_LAYERS, K + 1, D, D), dtype=jnp.float32) / np.sqrt(D)
        bias = jnp.zeros((NUM_LAYERS, D), dtype=jnp.float32)
        gamma = jnp.ones((NUM_LAYERS, D), dtype=jnp.float32)
        beta = jnp.zeros((NUM_LAYERS, D), dtype=jnp.float32)
        return {'node': node, 'edge_index': edge_index, 'edge_attr': edge_attr, 'batch_ptr': batch_ptr, 'W': W, 'bias': bias, 'gamma': gamma, 'beta': beta}
    _L3_gnn_all = _L3_gnn_setup()
    _L3_gnn_in = {k: v for k, v in _L3_gnn_all.items() if k in ('batch_ptr', 'W', 'bias', 'gamma', 'beta')}
    del _L3_gnn_all
    return {'x': x, 'src': src, 'dst': dst, 'edge_weight': edge_weight, 'L0_gnn_W1l': _L0_gnn_in['W1l'], 'L0_gnn_b1l': _L0_gnn_in['b1l'], 'L0_gnn_W1r': _L0_gnn_in['W1r'], 'L0_gnn_W2l': _L0_gnn_in['W2l'], 'L0_gnn_b2l': _L0_gnn_in['b2l'], 'L0_gnn_W2r': _L0_gnn_in['W2r'], 'L1_gnn_W_conv': _L1_gnn_in['W_conv'], 'L1_gnn_b_conv': _L1_gnn_in['b_conv'], 'L1_gnn_W_lin': _L1_gnn_in['W_lin'], 'L1_gnn_b_lin': _L1_gnn_in['b_lin'], 'L2_gnn_W1': _L2_gnn_in['W1'], 'L2_gnn_b1': _L2_gnn_in['b1'], 'L2_gnn_W2': _L2_gnn_in['W2'], 'L2_gnn_b2': _L2_gnn_in['b2'], 'L3_gnn_batch_ptr': _L3_gnn_in['batch_ptr'], 'L3_gnn_W': _L3_gnn_in['W'], 'L3_gnn_bias': _L3_gnn_in['bias'], 'L3_gnn_gamma': _L3_gnn_in['gamma'], 'L3_gnn_beta': _L3_gnn_in['beta']}

def reference(x, src, dst, edge_weight, L0_gnn_W1l, L0_gnn_b1l, L0_gnn_W1r, L0_gnn_W2l, L0_gnn_b2l, L0_gnn_W2r, L1_gnn_W_conv, L1_gnn_b_conv, L1_gnn_W_lin, L1_gnn_b_lin, L2_gnn_W1, L2_gnn_b1, L2_gnn_W2, L2_gnn_b2, L3_gnn_batch_ptr, L3_gnn_W, L3_gnn_bias, L3_gnn_gamma, L3_gnn_beta):
    import jax
    import jax.numpy as jnp

    def _L0_gnn_ref(x, edge_index, W1l, b1l, W1r, W2l, b2l, W2r):
        import jax, jax.numpy as jnp
        import numpy as np
        N = 6250
        E = 100000
        D_IN = 128
        D_HID = 128
        D_OUT = 128

        def _sage_conv(h, src, dst, Wl, bl, Wr):
            msgs = h[src]
            agg = jax.ops.segment_sum(msgs, dst, num_segments=N)
            deg = jax.ops.segment_sum(jnp.ones((src.shape[0],), h.dtype), dst, num_segments=N)
            agg = agg / jnp.maximum(deg, 1.0)[:, None]
            return agg @ Wl.T + bl + h @ Wr.T
        src, dst = (edge_index[0], edge_index[1])
        h = jax.nn.relu(_sage_conv(x, src, dst, W1l, b1l, W1r))
        return _sage_conv(h, src, dst, W2l, b2l, W2r)

    def _L1_gnn_ref(x, edge_index, W_conv, b_conv, W_lin, b_lin):
        import jax, jax.numpy as jnp
        import numpy as np
        N_NODES = 6250
        N_EDGES = 100000
        IN_DIM, HID_DIM, OUT_DIM = (128, 64, 128)

        def gcn_conv(x, edge_index, W, b):
            n = x.shape[0]
            loop = jnp.arange(n, dtype=edge_index.dtype)
            src = jnp.concatenate([edge_index[0], loop])
            dst = jnp.concatenate([edge_index[1], loop])
            deg = jax.ops.segment_sum(jnp.ones_like(dst, dtype=x.dtype), dst, num_segments=n)
            dinv = jnp.where(deg > 0, jax.lax.rsqrt(deg), 0.0)
            norm = dinv[src] * dinv[dst]
            h = x @ W
            msg = h[src] * norm[:, None]
            agg = jax.ops.segment_sum(msg, dst, num_segments=n)
            return agg + b
        h = gcn_conv(x, edge_index, W_conv, b_conv)
        h = jax.nn.relu(h)
        return h @ W_lin + b_lin

    def _L2_gnn_ref(x, edge_index, W1, b1, W2, b2):
        import jax, jax.numpy as jnp
        import numpy as np
        N_NODES = 6250

        def gcn_conv(x, edge_index, W, b):
            n = x.shape[0]
            h = x @ W
            loop = jnp.arange(n, dtype=edge_index.dtype)
            src = jnp.concatenate([edge_index[0], loop])
            dst = jnp.concatenate([edge_index[1], loop])
            deg = jax.ops.segment_sum(jnp.ones_like(dst, dtype=h.dtype), dst, num_segments=n)
            dinv = jnp.where(deg > 0, jax.lax.rsqrt(deg), 0.0)
            norm = dinv[src] * dinv[dst]
            msg = h[src] * norm[:, None]
            out = jax.ops.segment_sum(msg, dst, num_segments=n)
            return out + b
        h = jax.nn.relu(gcn_conv(x, edge_index, W1, b1))
        out = gcn_conv(h, edge_index, W2, b2)
        return out

    def _L3_gnn_ref(node, edge_index, edge_attr, batch_ptr, W, bias, gamma, beta):
        import jax, jax.numpy as jnp
        import numpy as np
        LN_EPS = 1e-05
        K = 3
        NUM_LAYERS = 3
        N = node.shape[0]
        src, dst = (edge_index[0], edge_index[1])
        deg = jax.ops.segment_sum(edge_attr, dst, num_segments=N)
        dinv = jnp.where(deg > 0, jax.lax.rsqrt(jnp.where(deg > 0, deg, 1.0)), 0.0)
        w = dinv[src] * edge_attr * dinv[dst]
        h = node
        for l in range(NUM_LAYERS):
            out = h @ W[l, 0]
            x = h
            for k in range(1, K + 1):
                x = jax.ops.segment_sum(w[:, None] * x[src], dst, num_segments=N)
                out = out + x @ W[l, k]
            out = out + bias[l]
            y = h + out
            mu = jnp.mean(y, axis=-1, keepdims=True)
            var = jnp.mean(jnp.square(y - mu), axis=-1, keepdims=True)
            y = (y - mu) * jax.lax.rsqrt(var + LN_EPS) * gamma[l] + beta[l]
            h = jax.nn.relu(y)
        return h
    edge_index = jnp.stack([src, dst])
    x = _layernorm(x + _L0_gnn_ref(x, edge_index, L0_gnn_W1l, L0_gnn_b1l, L0_gnn_W1r, L0_gnn_W2l, L0_gnn_b2l, L0_gnn_W2r), axis=-1)
    x = _layernorm(x + _L1_gnn_ref(x, edge_index, L1_gnn_W_conv, L1_gnn_b_conv, L1_gnn_W_lin, L1_gnn_b_lin), axis=-1)
    x = _layernorm(x + _L2_gnn_ref(x, edge_index, L2_gnn_W1, L2_gnn_b1, L2_gnn_W2, L2_gnn_b2), axis=-1)
    x = _layernorm(x + _L3_gnn_ref(x, edge_index, edge_weight, L3_gnn_batch_ptr, L3_gnn_W, L3_gnn_bias, L3_gnn_gamma, L3_gnn_beta), axis=-1)
    return x

_drawn_inputs = setup_inputs


def setup_inputs(seed=0):
    import zlib

    import numpy as np

    out = dict(_drawn_inputs(seed))
    spreads = {'L0_gnn_b1l': (0.0, 0.335),
     'L0_gnn_b2l': (0.0, 0.1),
     'L1_gnn_b_conv': (0.0, 0.1),
     'L1_gnn_b_lin': (0.0, 0.1),
     'L2_gnn_b1': (0.0, 0.1),
     'L2_gnn_b2': (0.0, 0.1),
     'L3_gnn_bias': (0.0, 0.1),
     'L3_gnn_gamma': (1.0, 0.2),
     'L3_gnn_beta': (0.0, 0.1)}
    factors = {'L0_gnn_W1l': 6.652}
    for name, (base, spread) in spreads.items():
        noise = np.random.default_rng([zlib.crc32(name.encode()), seed]).standard_normal(out[name].shape)
        drawn = base * np.exp(spread * noise) if base else spread * noise
        out[name] = jnp.asarray(drawn.astype(out[name].dtype))
    for name, factor in factors.items():
        out[name] = (out[name] * factor).astype(out[name].dtype)
    return out
```

```python
import concourse.bass as bass
from concourse import mybir
from contextlib import ExitStack

F32 = mybir.dt.float32
I32 = mybir.dt.int32
ALU = mybir.AluOpType
ACT = mybir.ActivationFunctionType

P = 128
N, D, E = 6250, 128, 106250
D1 = 64
TILES = -(-N // P)
LAST = N - (TILES - 1) * P
CHUNKS = 832
STEPS = CHUNKS + TILES - 1
CG = 7
FULL = E // P
REST = E - FULL * P
NQ = 16
RING = 64
SUB = 8
GT = 7
GROUPS = TILES // GT
PAD_DST = 1 << 20
EPS = 1e-5
HOPS = 3
LAYERS = 3
LINKS = 24
STAGES = 5
assert RING >= NQ + TILES - 1 and STEPS % (2 * SUB) == 0 and CHUNKS % RING == 0 and TILES % GT == 0

ROWS = ["L0_gnn_b1l", "L0_gnn_b2l", "L1_gnn_b_lin", "L2_gnn_b1", "L2_gnn_b2"]
SQUARE = ["L0_gnn_W1l", "L0_gnn_W1r", "L0_gnn_W2l", "L0_gnn_W2r"]


def program(nc, A, out):
    ctx = ExitStack()
    with ctx:
        def sb(name, shape, dt=F32):
            return ctx.enter_context(nc.sbuf_tensor(name, shape, dt))

        def pb(name, shape):
            return ctx.enter_context(nc.psum_tensor(name, shape, F32))

        def sem(name):
            return ctx.enter_context(nc.semaphore(name))

        table = nc.dram_tensor("table", (TILES * P, D), F32, kind="Internal").ap()
        dst_pad = nc.dram_tensor("dst_pad", (CG * P, P), F32, kind="Internal").ap()
        wgt_pad = nc.dram_tensor("wgt_pad", (CG * P, P), F32, kind="Internal").ap()

        xres = sb("xres", [P, TILES, D])
        hcur = sb("hcur", [P, TILES, D])
        outacc = sb("outacc", [P, TILES, D])
        acc = sb("acc", [P, TILES, D + 2])
        rcnt = sb("rcnt", [P, TILES])
        dinv = sb("dinv", [P, 2, TILES])
        dtmp = sb("dtmp", [P, 2, TILES])
        dmask = sb("dmask", [P, 2, TILES])
        src_idx = sb("src_idx", [P, CG * P], I32)
        dst_rel = sb("dst_rel", [P, CG * P])
        one_wgt = sb("one_wgt", [P, CG * P, 2])
        slot_row = sb("slot_row", [1, CG * P], I32)
        tile_row = sb("tile_row", [1, CG * P], I32)
        ring = sb("ring", [P, RING, D])
        stage = sb("stage", [P, RING], I32)
        hot = sb("hot", [P, 2 * SUB, P])
        zin = sb("zin", [P, 2 * GT, D])
        zT = sb("zT", [P, 2 * GT, P])
        tb = sb("tb", [P, GT, D])
        t = sb("t", [P, GT, D])
        stats = sb("stats", [P, GT, 6])
        mv = sb("mv", [P, GT, 2])
        sd = sb("sd", [P, GT])
        rstd = sb("rstd", [P, GT])
        wraw = sb("wraw", [P, 4, D])
        w0 = sb("w0", [P, 4, D])
        wc = sb("wc", [P, D1])
        wlin = sb("wlin", [D1, D])
        bc = sb("bc", [D1, 1])
        w2 = sb("w2", [P, 2, D])
        w3 = sb("w3", [P, LAYERS * (HOPS + 1), D])
        rows = sb("rows", [P, len(ROWS), D])
        rows3 = sb("rows3", [P, 3, LAYERS, D])
        ident = sb("ident", [P, P])
        ones = sb("ones", [P, P])
        iota_i = sb("iota_i", [P, P], I32)
        iota = sb("iota", [P, P])
        ci = sb("ci", [P, CG], I32)
        cf = sb("cf", [P, CG])
        number = sb("number", [P, CG])
        chunk_col = sb("chunk_col", [P, CG])
        chunk_idx = sb("chunk_idx", [P, CG], I32)
        base_col = sb("base_col", [P, CG])

        flat = hcur[:, :, :].rearrange("p t d -> p (t d)")
        ge = flat[:, 0:CG * STEPS].rearrange("p (k s) -> p k s", k=CG)
        oflat = outacc[:, :, :].rearrange("p t d -> p (t d)")
        step_f = oflat[:, 0:STEPS]
        step_i = oflat[:, 896:896 + STEPS].bitcast(I32)
        chunk_f = oflat[0:1, 1792:1792 + STEPS]
        chunk_i = oflat[0:1, 2688:2688 + STEPS].bitcast(I32)
        tile_f = oflat[0:1, 3584:3584 + STEPS]
        rflat = ring[:, :, :].rearrange("p r d -> p (r d)")
        dnat_i = rflat[:, 0:896].bitcast(I32).rearrange("p (k e) -> p k e", k=CG)
        snat_i = rflat[:, 896:1792].bitcast(I32).rearrange("p (k e) -> p k e", k=CG)
        wnat = rflat[:, 1792:2688].rearrange("p (k e) -> p k e", k=CG)
        dnat = rflat[:, 2688:3584].rearrange("p (k e) -> p k e", k=CG)
        snat = rflat[:, 3584:4480].rearrange("p (k e) -> p k e", k=CG)
        dstep = rflat[:, 4480:5376].rearrange("p (k e) -> p k e", k=CG)
        wstep = rflat[:, 5376:6272].rearrange("p (k e) -> p k e", k=CG)

        pstep = [pb(f"pstep{i}", [P, 512]) for i in range(2)]
        pT = pb("pT", [P, 2048])
        pO = pb("pO", [P, 1024])

        def names(text):
            return [sem(n) for n in text.split()]

        (in_edges, in_x, in_w, g_const, v_nat, pad_out, p_walk, v_walk, walk_dma, v_steps, p_tabs, v_tabs,
         v_chain, a_deg) = names(
            "in_edges in_x in_w g_const v_nat pad_out p_walk v_walk walk_dma v_steps p_tabs v_tabs v_chain a_deg")
        landed = [sem(f"landed{q}") for q in range(NQ)]
        idx_staged, pe_step, hot_ready, acc_done, scales_ready = names(
            "idx_staged pe_step hot_ready acc_done scales_ready")
        (z_ready, zt_ps, zt_ready, h64_ps, h64_ready, o_ps, post_done, tb_ready, tb_sent, tb_free,
         table_done, var_ready, sd_ready, out_done, credits) = names(
            "z_ready zt_ps zt_ready h64_ps h64_ready o_ps post_done tb_ready tb_sent tb_free "
            "table_done var_ready sd_ready out_done credits")
        v_group = sem("v_group")
        pool_go, pe_go, act_go, dve_go, sp_go = names("pool_go pe_go act_go dve_go sp_go")

        STEP0 = RING
        table_v = table.rearrange("(t p) d -> p t d", p=P)
        out_v = out[0:(TILES - 1) * P, :].rearrange("(t p) d -> p t d", p=P)

        def stages(eng, stage_of):
            for a in range(STAGES):
                stage_of(a, a, None)
            with eng.Fori(0, LAYERS) as layer:
                for k in range(HOPS):
                    stage_of(layer * HOPS + (STAGES + k), "hop" + str(k + 1), layer)

        def uses_h(kind):
            return kind in (0, 1, "hop1")

        block = ctx.enter_context(nc.Block())

        @block.sync
        def _(sp):
            d, s, w = A["dst"], A["src"], A["edge_weight"]
            sp.wait_ge(v_nat, 3)
            for nat, a in ((dnat_i, d), (snat_i, s), (wnat, w)):
                k6 = 6 * P
                sp.dma_start(nat[:, 0:6, :], a[0:k6 * P].rearrange("(k p e) -> p k e", p=P, e=P)).then_inc(in_edges, 16)
                sp.dma_start(nat[0:FULL - k6, 6, :], a[k6 * P:FULL * P].rearrange("(p e) -> p e", e=P)).then_inc(in_edges, 16)
                sp.dma_start(nat[FULL - k6:FULL - k6 + 1, 6, 0:REST],
                             a[FULL * P:E].rearrange("(p e) -> p e", p=1)).then_inc(in_edges, 16)
            sp.dma_start(xres[:, 0:TILES - 1, :],
                         A["x"][0:(TILES - 1) * P, :].rearrange("(t p) d -> p t d", p=P)).then_inc(in_x, 16)
            sp.dma_start(xres[0:LAST, TILES - 1, :], A["x"][(TILES - 1) * P:N, :]).then_inc(in_x, 16)
            sp.wait_ge(v_nat, 5)
            sp.dma_start(dst_pad.rearrange("(k p) e -> p k e", p=P), dnat).then_inc(pad_out, 16)
            sp.dma_start(wgt_pad.rearrange("(k p) e -> p k e", p=P), wnat).then_inc(pad_out, 16)

            def dense(a, kind, layer):
                def group(g):
                    sp.wait_ge(tb_ready, a * GROUPS + g + 1)
                    sp.sem_inc(sp_go, 1)
                    sp.dma_start(table_v[:, bass.ds(g * GT, GT), :], tb[:, :, :]).then_inc(table_done, 16)
                    sp.wait_ge(table_done, (a * GROUPS + g + 1) * 16)
                    sp.sem_inc(tb_free, 1)
                with sp.Fori(0, GROUPS) as g:
                    group(g)
            stages(sp, dense)
            for g in range(GROUPS):
                sp.wait_ge(tb_ready, (STAGES + LAYERS * HOPS) * GROUPS + g + 1)
                lo, hi = g * GT, (g + 1) * GT
                n = GT if hi < TILES else GT - 1
                sp.dma_start(out_v[:, lo:lo + n, :], tb[:, 0:n, :]).then_inc(out_done, 16)
                if n < GT:
                    sp.dma_start(out[(TILES - 1) * P:N, :], tb[0:LAST, GT - 1, :]).then_inc(out_done, 16)
                sp.wait_ge(out_done, (g + 1) * 16 + 16 * (n < GT))
                sp.sem_inc(tb_free, 1)

        @block.gpsimd
        def _(pool):
            pool.iota(iota_i[:, :], pattern=[[1, P]], base=0, channel_multiplier=0).then_inc(g_const, 1)
            pool.iota(ci[:, :], pattern=[[P, CG]], base=0, channel_multiplier=1).then_inc(g_const, 1)
            pool.iota(step_i, pattern=[[1, STEPS]], base=0, channel_multiplier=0).then_inc(g_const, 1)
            pool.memset(ones[:, :], 1.0).then_inc(g_const, 1)
            pool.memset(ident[:, :], 0.0).then_inc(g_const, 1)
            pool.wait_ge(g_const, 5)
            pool.affine_select(out=ident[:, :], in_=ident[:, :], compare_op=ALU.not_equal, fill=1.0, base=0,
                               pattern=[[-1, P]], channel_multiplier=1).then_inc(g_const, 1)
            pool.wait_ge(pad_out, 32)
            pool.wait_ge(v_walk, 1)
            for k in range(CG):
                for rows_, pad in ((dstep, dst_pad), (wstep, wgt_pad)):
                    pool.indirect_dma_start(out=rows_[:, k, :], out_offset=None, in_=pad[:, :],
                                            in_offset=bass.IndirectOffsetOnAxis(ap=chunk_idx[:, k:k + 1], axis=0)
                                            ).then_inc(walk_dma, 16)

            def gather(a, kind, layer):
                src = A["x"] if kind == 0 else table
                if kind == 0:
                    pool.wait_ge(v_tabs, 1)
                else:
                    pool.wait_ge(table_done, a * (GROUPS * 16))
                    pool.sem_inc(pool_go, 1)
                with pool.Fori(0, CHUNKS // RING) as it:
                    for s in range(0, RING, SUB):
                        pool.wait_ge(pe_step, a * STEPS + it * RING + (STEP0 + s + SUB - NQ))
                        if s % NQ == 0:
                            pool.wait_ge(idx_staged, a * (CHUNKS // NQ) + it * (RING // NQ) + (s // NQ + 1))
                        pool.sem_inc(pool_go, 1)
                        for c in range(s, s + SUB):
                            pool.indirect_dma_start(out=ring[:, c, :], out_offset=None, in_=src[:, :],
                                                    in_offset=bass.IndirectOffsetOnAxis(ap=stage[:, c:c + 1], axis=0)
                                                    ).then_inc(landed[c % NQ], 16)
            stages(pool, gather)

        @block.scalar
        def _(act):
            for i, n in enumerate(SQUARE):
                act.dma_start(wraw[:, i, :], A[n]).then_inc(in_w, 16)
            act.dma_start(wc[:, :], A["L1_gnn_W_conv"]).then_inc(in_w, 16)
            act.dma_start(wlin[:, :], A["L1_gnn_W_lin"]).then_inc(in_w, 16)
            act.dma_start(bc[:, :], A["L1_gnn_b_conv"].rearrange("(n a) -> n a", a=1)).then_inc(in_w, 16)
            act.dma_start(w2[:, 0, :], A["L2_gnn_W1"]).then_inc(in_w, 16)
            act.dma_start(w2[:, 1, :], A["L2_gnn_W2"]).then_inc(in_w, 16)
            act.dma_start(w3[:, :, :], A["L3_gnn_W"].rearrange("l k i o -> i (l k) o")).then_inc(in_w, 16)
            for i, n in enumerate(ROWS):
                act.dma_start(rows[:, i, :], A[n].partition_broadcast(P)).then_inc(in_w, 16)
            for i, n in enumerate(("bias", "gamma", "beta")):
                act.dma_start(rows3[:, i, :, :], A["L3_gnn_" + n].partition_broadcast(P)).then_inc(in_w, 16)

            def dense(a, kind, layer):
                if kind == 0:
                    act.wait_ge(v_tabs, 1)
                with act.Fori(0, CHUNKS // RING) as it:
                    for q in range(RING // NQ):
                        act.wait_ge(pe_step, a * STEPS + it * RING + (STEP0 + (q + 1) * NQ - RING))
                        act.sem_inc(act_go, 1)
                        act.activation(stage[:, q * NQ:(q + 1) * NQ], src_idx[:, bass.ds(it * RING + q * NQ, NQ)],
                                       ACT.Copy).then_inc(idx_staged, 1)
                if kind == 0:
                    act.wait_ge(v_steps, 2)
                    act.activation(dtmp[:, :, :], dtmp[:, :, :], ACT.Sqrt).then_inc(a_deg, 1)
                n = 2 * GT if uses_h(kind) else GT
                with act.Fori(0, GROUPS) as g:
                    act.wait_ge(zt_ps, a * GROUPS + g + 1)
                    act.sem_inc(act_go, 1)
                    for lo in range(0, n, 4):
                        hi = min(lo + 4, n)
                        last = act.activation(zT[:, lo:hi, :].rearrange("p t n -> p (t n)"),
                                              pT[:, lo * P:hi * P], ACT.Copy)
                    last.then_inc(zt_ready, 1)
                    if kind == 2:
                        act.wait_ge(h64_ps, g + 1)
                        act.sem_inc(act_go, 1)
                        for lo, hi in ((0, 4), (4, 7)):
                            last = act.activation(zT[0:D1, GT + lo:GT + hi, :].rearrange("p t n -> p (t n)"),
                                                  pT[0:D1, lo * P:hi * P], ACT.Relu, bias=bc[:, :])
                        last.then_inc(h64_ready, 1)
                    norm = {1: 0, 2: 1, 4: 2}.get(kind)
                    if norm is not None:
                        root(act, norm * GROUPS + g)
                    if kind == "hop3":
                        root(act, (layer + 3) * GROUPS + g)

            def root(act, n):
                act.wait_ge(var_ready, n + 1)
                act.sem_inc(act_go, 1)
                act.activation(sd[:, :], sd[:, :], ACT.Sqrt).then_inc(sd_ready, 1)
            stages(act, dense)
            with act.Fori(0, GROUPS) as g:
                root(act, g + (3 + LAYERS) * GROUPS)

        @block.tensor
        def _(pe):
            pe.wait_ge(g_const, 6)
            pe.wait_ge(p_walk, 1)
            for half in range(2):
                for k in range(CG):
                    pe.matmul(pT[:, half * 512:half * 512 + STEPS // 2], ones[:, :],
                              ge[:, k, half * (STEPS // 2):(half + 1) * (STEPS // 2)], start=(k == 0), stop=(k == CG - 1))
            for s in range(CG):
                n = min(P, STEPS - s * P)
                for k in range(CG):
                    last = pe.matmul(pT[0:n, 1024 + s:1025 + s], ge[:, k, s * P:s * P + n], ones[:, 0:1],
                                     start=(k == 0), stop=(k == CG - 1))
            last.then_inc(p_tabs, 1)
            pe.wait_ge(v_nat, 5)
            for k in range(CG):
                last = pe.transpose(pO[:, k * P:(k + 1) * P], snat[:, k, :], ident[:, :])
            last.then_inc(p_tabs, 1)
            pe.wait_ge(in_w, 16 * (10 + len(ROWS) + 3))
            for i in range(4):
                last = pe.transpose(pstep[0][:, i * P:(i + 1) * P], wraw[:, i, :], ident[:, :])
            last.then_inc(p_tabs, 1)
            pe.wait_ge(v_walk, 2)
            for k in range(CG):
                last = pe.transpose(pT[:, k * P:(k + 1) * P], dstep[:, k, :], ident[:, :])
            last.then_inc(p_tabs, 1)
            for k in range(CG):
                last = pe.transpose(pT[:, 1024 + k * P:1024 + (k + 1) * P], wstep[:, k, :], ident[:, :])
            last.then_inc(p_tabs, 1)
            pe.sem_inc(pe_step, STEP0)
            slots = [pe.alloc_register(f"pe_slot{j}") for j in range(SUB)]

            def walk(a, kind, wait_gathers, lo, hi):
                with pe.Fori(lo, hi) as it:
                    for h in range(2):
                        for q in (0, 4):
                            pe.load(slots[q:q + 4], slot_row[0:1, bass.ds(it * (2 * SUB) + (h * SUB + q), 4)])
                        pe.wait_ge(hot_ready, a * (STEPS // SUB) + it * 2 + (h + 1))
                        pe.sem_inc(pe_go, 1)
                        for j in range(SUB):
                            slot = pe.snap(slots[j], min_val=0, max_val=RING - 1)
                            if wait_gathers:
                                pe.wait_ge(landed[h * SUB + j], (a * (CHUNKS // NQ) + it + 1) * 16)
                            pe.wait_ge(acc_done, a * (STEPS + 1) + it * (2 * SUB) + (h * SUB + j + 1))
                            mm = pe.matmul(pstep[j % 2][:, 0:D], hot[:, h * SUB + j, :],
                                           ring[:, bass.ds(slot, 1), :], start=True, stop=True)
                            if kind == 0:
                                mm = pe.matmul(pstep[j % 2][:, D:D + 2], hot[:, h * SUB + j, :],
                                               one_wgt[:, bass.ds(it * (2 * SUB) + (h * SUB + j), 1), :],
                                               start=True, stop=True)
                            mm.then_inc(pe_step, 1)

            def dense(a, kind, layer):
                if kind == 0:
                    pe.wait_ge(v_tabs, 1)
                walk(a, kind, True, 0, CHUNKS // NQ)
                walk(a, kind, False, CHUNKS // NQ, STEPS // NQ)
                n = 2 * GT if uses_h(kind) else GT
                with pe.Fori(0, GROUPS) as g:
                    pe.wait_ge(z_ready, a * GROUPS + g + 1)
                    pe.sem_inc(pe_go, 1)
                    for j in range(n):
                        last = pe.transpose(pT[:, j * P:(j + 1) * P], zin[:, j, :], ident[:, :])
                    last.then_inc(zt_ps, 1)
                    pe.wait_ge(zt_ready, a * GROUPS + g + 1)
                    pe.wait_ge(post_done, a * GROUPS + g + 1)
                    pe.sem_inc(pe_go, 1)
                    if kind == 2:
                        zf = zT[:, 0:GT, :].rearrange("p t n -> p (t n)")
                        for lo, hi in ((0, 512), (512, GT * P)):
                            last = pe.matmul(pT[0:D1, lo:hi], wc[:, :], zf[:, lo:hi], start=True, stop=True)
                        last.then_inc(h64_ps, 1)
                        pe.wait_ge(h64_ready, g + 1)
                        pe.sem_inc(pe_go, 1)
                    for j in range(GT):
                        o = pO[:, j * P:(j + 1) * P]
                        z, h = zT[:, j, :], zT[:, GT + j, :]
                        if kind in (0, 1):
                            last = pe.matmul(o, z, w0[:, 2 * kind, :], start=True, stop=False)
                            last = pe.matmul(o, h, w0[:, 2 * kind + 1, :], start=False, stop=True)
                        elif kind == 2:
                            last = pe.matmul(o, zT[0:D1, GT + j, :], wlin[:, :], start=True, stop=True)
                        elif kind in (3, 4):
                            last = pe.matmul(o, z, w2[:, kind - 3, :], start=True, stop=True)
                        else:
                            k = int(kind[3])
                            if k == 1:
                                pe.matmul(o, h, w3[:, bass.ds(layer * (HOPS + 1), 1), :], start=True, stop=False)
                            last = pe.matmul(o, z, w3[:, bass.ds(layer * (HOPS + 1) + k, 1), :],
                                             start=(k != 1), stop=True)
                    last.then_inc(o_ps, 1)
            stages(pe, dense)

        @block.vector
        def _(dve):
            V = nc.vector
            count = [0]

            def link(ins):
                count[0] += 1
                ins.then_inc(v_chain, 1)
                dve.wait_ge(v_chain, count[0])

            V.memset(xres[:, TILES - 1, :], 0.0)
            V.memset(dnat_i, PAD_DST).then_inc(v_nat, 1)
            V.memset(snat_i, 0).then_inc(v_nat, 1)
            V.memset(wnat, 0.0).then_inc(v_nat, 1)
            V.memset(one_wgt[:, :, 0:1], 1.0)
            V.memset(chunk_idx[:, :], 0)
            dve.sem_inc(post_done, 1)
            dve.sem_inc(tb_free, 1)
            dve.sem_inc(acc_done, 1)
            link(V.memset(chunk_col[:, :], 1.0))
            dve.wait_ge(in_edges, 144)
            V.tensor_copy(dnat, dnat_i).then_inc(v_nat, 1)
            V.tensor_copy(snat, snat_i).then_inc(v_nat, 1)
            dve.wait_ge(g_const, 6)
            V.tensor_copy(iota[:, :], iota_i[:, :])
            V.tensor_copy(step_f, step_i)
            link(V.tensor_copy(number[:, :], ci[:, :]))
            link(V.tensor_single_scalar(ci[:, :], dnat_i[:, :, 0], 7, ALU.arith_shift_right))
            link(V.tensor_copy(base_col[:, :], ci[:, :]))
            link(V.memset(base_col[0:1, 0:1], 0.0))
            link(V.tensor_scalar(base_col[:, :], base_col[:, :], float(TILES - 1), None, ALU.min))
            link(V.tensor_tensor(cf[:, :], number[:, :], base_col[:, :], ALU.add))
            for k in range(CG):
                last = V.tensor_scalar(ge[:, k, :], step_f, cf[:, k:k + 1], None, ALU.is_ge)
            last.then_inc(p_walk, 1)
            dve.wait_ge(p_tabs, 1)
            half = STEPS // 2
            for s in range(2):
                V.tensor_scalar(chunk_f[:, s * half:(s + 1) * half], pT[0:1, s * 512:s * 512 + half], -1.0, None, ALU.add)
            V.tensor_copy(chunk_col[:, 0:CG - 1], pT[:, 1024:1024 + CG - 1])
            tail = STEPS - (CG - 1) * P
            link(V.tensor_copy(chunk_col[0:tail, CG - 1:CG], pT[0:tail, 1024 + CG - 1:1024 + CG]))
            link(V.tensor_scalar(chunk_col[:, :], chunk_col[:, :], -1.0, None, ALU.add))
            V.tensor_copy(chunk_idx[:, :], chunk_col[:, :]).then_inc(v_walk, 1)
            link(V.tensor_tensor(tile_f, step_f[0:1, :], chunk_f, ALU.subtract))
            V.tensor_copy(tile_row[:, 0:STEPS], tile_f)
            link(V.tensor_copy(chunk_i, chunk_f))
            V.tensor_single_scalar(slot_row[:, 0:STEPS], chunk_i, RING - 1, ALU.bitwise_and)
            link(V.tensor_tensor(base_col[:, :], number[:, :], chunk_col[:, :], ALU.subtract))
            link(V.tensor_scalar(base_col[:, :], base_col[:, :], float(P), None, ALU.mult))
            dve.wait_ge(walk_dma, 16 * 2 * CG)
            for k in range(CG):
                last = V.tensor_scalar(dstep[:, k, :], dstep[:, k, :], base_col[:, k:k + 1], None, ALU.subtract)
            last.then_inc(v_walk, 1)
            dve.wait_ge(p_tabs, 2)
            V.tensor_copy(src_idx[:, :], pO[:, 0:CG * P])
            dve.wait_ge(p_tabs, 3)
            V.tensor_copy(w0[:, :, :].rearrange("p w d -> p (w d)"), pstep[0][:, :])
            dve.wait_ge(p_tabs, 5)
            V.tensor_copy(dst_rel[:, :], pT[:, 0:CG * P])
            link(V.tensor_copy(one_wgt[:, :, 1], pT[:, 1024:1024 + CG * P]))
            dve.wait_ge(in_x, 32)
            dve.sem_inc(v_tabs, 1)
            tiles = [dve.alloc_register(f"dve_tile{j}") for j in range(SUB)]

            def walk(a, kind):
                width = D + 2 if kind == 0 else D
                weighted = isinstance(kind, str)
                if kind in (2, 3, 4):
                    dve.sem_inc(acc_done, 1)
                else:
                    V.memset(acc[:, :, 0:width], 0.0).then_inc(acc_done, 1)
                with dve.Fori(0, STEPS // (2 * SUB)) as it:
                    for h in range(2):
                        for q in (0, 4):
                            dve.load(tiles[q:q + 4], tile_row[0:1, bass.ds(it * (2 * SUB) + (h * SUB + q), 4)])
                        for j in range(SUB):
                            i = it * (2 * SUB) + (h * SUB + j)
                            if weighted:
                                last = V.tensor_scalar(hot[:, h * SUB + j, :], iota[:, :], dst_rel[:, bass.ds(i, 1)],
                                                       one_wgt[:, bass.ds(i, 1), 1], ALU.is_equal, ALU.mult)
                            else:
                                last = V.tensor_scalar(hot[:, h * SUB + j, :], iota[:, :], dst_rel[:, bass.ds(i, 1)],
                                                       None, ALU.is_equal)
                        last.then_inc(hot_ready, 1)
                        for j in range(SUB):
                            tile = dve.snap(tiles[j], min_val=0, max_val=TILES - 1)
                            i = it * (2 * SUB) + (h * SUB + j)
                            dve.wait_ge(pe_step, a * STEPS + i + (STEP0 + 1))
                            dve.wait_ge(acc_done, a * (STEPS + 1) + i + 2)
                            to = acc[:, bass.ds(tile, 1), 0:D]
                            ins = V.tensor_tensor(to, to, pstep[j % 2][:, 0:D].rearrange("p (a d) -> p a d", a=1),
                                                  ALU.add)
                            if kind == 0:
                                to = acc[:, bass.ds(tile, 1), D:D + 2]
                                ins = V.tensor_tensor(to, to, pstep[j % 2][:, D:D + 2].rearrange("p (a d) -> p a d", a=1), ALU.add)
                            ins.then_inc(acc_done, 1)
                dve.wait_ge(acc_done, a * (STEPS + 1) + (STEPS + 2))
                dve.sem_inc(dve_go, 1)

            def degrees():
                link(V.tensor_scalar(rcnt[:, :], acc[:, :, D], 1.0, None, ALU.max))
                link(V.reciprocal(rcnt[:, :], rcnt[:, :]))
                link(V.tensor_scalar(acc[:, :, D], acc[:, :, D], 1.0, None, ALU.add))
                d2 = acc[:, :, D:D + 2].rearrange("p t c -> p c t")
                link(V.tensor_scalar(dmask[:, :, :], d2, 0.0, None, ALU.is_gt))
                link(V.tensor_scalar(dinv[:, :, :], dmask[:, :, :], -1.0, 1.0, ALU.mult, ALU.add))
                link(V.tensor_tensor(dtmp[:, :, :], d2, dmask[:, :, :], ALU.mult))
                link(V.tensor_tensor(dtmp[:, :, :], dtmp[:, :, :], dinv[:, :, :], ALU.add))
                dve.sem_inc(v_steps, 2)
                dve.wait_ge(a_deg, 1)
                link(V.reciprocal(dinv[:, :, :], dtmp[:, :, :]))
                link(V.tensor_tensor(dinv[:, :, :], dinv[:, :, :], dmask[:, :, :], ALU.mult))

            def wide(col):
                return col.broadcast_to([P, GT, D])

            def column(x):
                return x.rearrange("p (t a) -> p t a", a=1)

            def dense(a, kind, layer):
                walk(a, kind)
                if kind == 0:
                    degrees()
                scale = rcnt[:, :] if kind in (0, 1) else dinv[:, 0, :] if kind in (2, 3, 4) else dinv[:, 1, :]
                after = None if kind in (0,) else dinv[:, 0, :] if kind in (1, 2, 3) else dinv[:, 1, :]
                start = [0]
                with dve.Fori(0, GROUPS) as g:
                    G = a * GROUPS + g

                    def chained(ins):
                        start[0] += 1
                        ins.then_inc(v_group, 1)
                        dve.wait_ge(v_group, G * LINKS + start[0])
                        dve.sem_inc(dve_go, 1)
                    sl = bass.ds(g * GT, GT)
                    ins = V.tensor_tensor(zin[:, 0:GT, :], acc[:, sl, 0:D], wide(column(scale[:, sl])), ALU.mult)
                    if uses_h(kind):
                        ins = V.tensor_copy(zin[:, GT:2 * GT, :], (xres if kind == 0 else hcur)[:, sl, :])
                    chained(ins)
                    dve.sem_inc(z_ready, 1)
                    if kind in ("hop1", "hop2"):
                        dve.wait_ge(tb_free, G + 1)
                        dve.sem_inc(dve_go, 1)
                        V.tensor_tensor(tb[:, :, :], zin[:, 0:GT, :], wide(column(after[:, sl])), ALU.mult).then_inc(tb_ready, 1)
                    dve.wait_ge(o_ps, G + 1)
                    dve.sem_inc(dve_go, 1)
                    po = pO[:, 0:GT * P].rearrange("p (t d) -> p t d", t=GT)
                    if kind == "hop1":
                        V.tensor_copy(outacc[:, sl, :], po).then_inc(post_done, 1)
                    elif kind == "hop2":
                        V.tensor_tensor(outacc[:, sl, :], outacc[:, sl, :], po, ALU.add).then_inc(post_done, 1)
                    else:
                        if layer is None:
                            row = rows[:, kind:kind + 1, :]
                        else:
                            row = rows3[:, 0, bass.ds(layer, 1), :]
                        chained(V.tensor_tensor(t[:, :, :], po, row.broadcast_to([P, GT, D]), ALU.add))
                        dve.sem_inc(post_done, 1)
                        if kind in (0, 3):
                            chained(V.tensor_scalar(hcur[:, sl, :], t[:, :, :], 0.0, None, ALU.max))
                            new = hcur
                        else:
                            if kind == "hop3":
                                chained(V.tensor_tensor(t[:, :, :], t[:, :, :], outacc[:, sl, :], ALU.add))
                                res = hcur
                            else:
                                res = xres
                            chained(V.tensor_tensor(t[:, :, :], t[:, :, :], res[:, sl, :], ALU.add))
                            ln = {1: 0, 2: 1, 4: 2}.get(kind)
                            n = ln * GROUPS + g if ln is not None else (layer + 3) * GROUPS + g
                            normalise(n, chained)
                            if kind == "hop3":
                                chained(V.tensor_tensor(t[:, :, :], t[:, :, :],
                                                        rows3[:, 1, bass.ds(layer, 1), :].broadcast_to([P, GT, D]), ALU.mult))
                                chained(V.tensor_tensor(t[:, :, :], t[:, :, :],
                                                        rows3[:, 2, bass.ds(layer, 1), :].broadcast_to([P, GT, D]), ALU.add))
                                chained(V.tensor_scalar(hcur[:, sl, :], t[:, :, :], 0.0, None, ALU.max))
                                new = hcur
                            else:
                                chained(V.tensor_copy(xres[:, sl, :], t[:, :, :]))
                                if kind == 4:
                                    chained(V.tensor_copy(hcur[:, sl, :], t[:, :, :]))
                                new = xres
                        dve.wait_ge(tb_free, G + 1)
                        dve.sem_inc(dve_go, 1)
                        if after is None:
                            V.tensor_copy(tb[:, :, :], new[:, sl, :]).then_inc(tb_ready, 1)
                        else:
                            if kind in (1, 2, 3):
                                chained(V.tensor_tensor(acc[:, sl, 0:D], new[:, sl, :], wide(column(after[:, sl])), ALU.mult))
                            V.tensor_tensor(tb[:, :, :], new[:, sl, :], wide(column(after[:, sl])), ALU.mult).then_inc(tb_ready, 1)
                    dve.wait_ge(tb_ready, G + 1)
                    dve.wait_ge(post_done, G + 2)
                    dve.sem_inc(dve_go, 1)
                    dve.sem_inc(v_group, LINKS - start[0])
                assert start[0] < LINKS

            def normalise(n, chained):
                for j in range(GT):
                    ins = V.bn_stats(stats[:, j, :], t[:, j, :])
                chained(ins)
                for j in range(GT):
                    ins = V.bn_aggr(mv[:, j, :], stats[:, j, :])
                chained(ins)
                chained(V.tensor_scalar(sd[:, :], mv[:, :, 1], EPS, None, ALU.add))
                dve.sem_inc(var_ready, 1)
                dve.wait_ge(sd_ready, n + 1)
                dve.sem_inc(dve_go, 1)
                chained(V.reciprocal(rstd[:, :], sd[:, :]))
                for j in range(GT):
                    ins = V.tensor_scalar(t[:, j, :], t[:, j, :], mv[:, j, 0:1], rstd[:, j:j + 1], ALU.subtract, ALU.mult)
                chained(ins)

            stages(dve, dense)
            start = [0]
            total = STAGES + LAYERS * HOPS
            with dve.Fori(0, GROUPS) as g:
                G = g + total * GROUPS

                def chained(ins):
                    start[0] += 1
                    ins.then_inc(v_group, 1)
                    dve.wait_ge(v_group, G * LINKS + start[0])
                    dve.sem_inc(dve_go, 1)
                sl = bass.ds(g * GT, GT)
                chained(V.tensor_tensor(t[:, :, :], xres[:, sl, :], hcur[:, sl, :], ALU.add))
                normalise(g + (3 + LAYERS) * GROUPS, chained)
                dve.wait_ge(tb_free, G + 1)
                dve.sem_inc(dve_go, 1)
                V.tensor_copy(tb[:, :, :], t[:, :, :]).then_inc(tb_ready, 1)
                dve.wait_ge(tb_ready, G + 1)
                dve.sem_inc(v_group, LINKS - start[0])


_INS = ["x", "src", "dst", "edge_weight", "L0_gnn_W1l", "L0_gnn_b1l", "L0_gnn_W1r", "L0_gnn_W2l", "L0_gnn_b2l",
        "L0_gnn_W2r", "L1_gnn_W_conv", "L1_gnn_b_conv", "L1_gnn_W_lin", "L1_gnn_b_lin", "L2_gnn_W1", "L2_gnn_b1",
        "L2_gnn_W2", "L2_gnn_b2", "L3_gnn_W", "L3_gnn_bias", "L3_gnn_gamma", "L3_gnn_beta"]


def kernel(**inputs):
    import numpy as np
    import concourse.bacc as bacc
    from concourse.bass_utils import run_bass_kernel_spmd

    nc = bacc.Bacc("TRN2", target_bir_lowering=False, num_devices=1)
    arrays, A = {}, {}
    for name in _INS:
        a = np.ascontiguousarray(inputs[name])
        arrays[f"in_{name}"] = a
        A[name] = nc.dram_tensor(f"in_{name}", a.shape, mybir.dt.from_np(a.dtype), kind="ExternalInput").ap()
    out = nc.dram_tensor("out", (N, D), F32, kind="ExternalOutput").ap()
    program(nc, A, out)
    r = run_bass_kernel_spmd(nc, [arrays], core_ids=[0])
    return r.results[0]["out"]
```

```python
import concourse.bass as bass
from concourse import mybir
from contextlib import ExitStack

F32 = mybir.dt.float32
I32 = mybir.dt.int32
ALU = mybir.AluOpType
ACT = mybir.ActivationFunctionType

P = 128
N, D, E = 6250, 128, 106250
D1 = 64
TILES = -(-N // P)
LAST = N - (TILES - 1) * P
CHUNKS = 832
STEPS = CHUNKS + TILES - 1
CG = 7
FULL = E // P
REST = E - FULL * P
NQ = 16
RING = 64
SUB = 8
GT = 7
GROUPS = TILES // GT
PAD_DST = 1 << 20
EPS = 1e-5
HOPS = 3
LAYERS = 3
LINKS = 24
STAGES = 5
assert RING >= NQ + TILES - 1 and STEPS % (2 * SUB) == 0 and CHUNKS % RING == 0 and TILES % GT == 0

C0 = 432
T0 = 25
TEND = 31
WALK = C0 + TEND + 1
WIDE = (TILES - T0) * P
EDGE0 = C0 * P
LANE = (CHUNKS - C0) * P // P
QS = 8
LAP = LANE // QS
PAD_SRC = N + 10
SWEEP = 24
assert WALK % (2 * SUB) == 0 and C0 % NQ == 0 and WIDE == 3072 and 2 * SWEEP + 1 == TILES and LANE % QS == 0

ROWS = ["L0_gnn_b1l", "L0_gnn_b2l", "L1_gnn_b_lin", "L2_gnn_b1", "L2_gnn_b2"]
SQUARE = ["L0_gnn_W1l", "L0_gnn_W1r", "L0_gnn_W2l", "L0_gnn_W2r"]


def program(nc, A, out):
    ctx = ExitStack()
    with ctx:
        def sb(name, shape, dt=F32):
            return ctx.enter_context(nc.sbuf_tensor(name, shape, dt))

        def pb(name, shape):
            return ctx.enter_context(nc.psum_tensor(name, shape, F32))

        def sem(name):
            return ctx.enter_context(nc.semaphore(name))

        table = nc.dram_tensor("table", (TILES * P, D), F32, kind="Internal").ap()
        dst_pad = nc.dram_tensor("dst_pad", (CG * P, P), F32, kind="Internal").ap()
        wgt_pad = nc.dram_tensor("wgt_pad", (CG * P, P), F32, kind="Internal").ap()
        src_pad = nc.dram_tensor("src_pad", (CG * P, P), F32, kind="Internal").ap()
        counts = nc.dram_tensor("counts", (TILES * P, WIDE), F32, kind="Internal").ap()
        weights = nc.dram_tensor("weights", (TILES * P, WIDE), F32, kind="Internal").ap()
        x_kept = nc.dram_tensor("x_kept", (TILES, P, D), F32, kind="Internal").ap().rearrange("t p d -> p t d")

        xres = sb("xres", [P, TILES, D])
        hcur = sb("hcur", [P, TILES, D])
        outacc = xres
        acc = sb("acc", [P, TILES, D])
        degs = sb("degs", [P, TILES, 2])
        rcnt = sb("rcnt", [P, TILES])
        dinv = sb("dinv", [P, 2, TILES])
        dtmp = sb("dtmp", [P, 2, TILES])
        dmask = sb("dmask", [P, 2, TILES])
        src_idx = sb("src_idx", [P, CG * P], I32)
        dst_rel = sb("dst_rel", [P, CG * P])
        wgt = sb("wgt", [P, CG * P])
        tail_mask = sb("tail_mask", [P, WALK - C0])
        flag = sb("flag", [1, 4])
        flag_i = sb("flag_i", [1, 4], I32)
        first_dst = sb("first_dst", [1, 1], I32)
        same = sb("same", [P, 1])
        matrix = sb("matrix", [P, 2, WIDE])
        hrow = sb("hrow", [P, 2, D])
        lane_i = sb("lane_i", [P, 2, QS], I32)
        lane_w = sb("lane_w", [P, 2, QS])
        lane_1 = sb("lane_1", [P, 2, QS])
        slot_row = sb("slot_row", [1, CG * P], I32)
        tile_row = sb("tile_row", [1, CG * P], I32)
        ring = sb("ring", [P, RING, D])
        stage = sb("stage", [P, RING], I32)
        hot = sb("hot", [P, 2 * SUB, P])
        zz = sb("zz", [P, 4 * GT, D])
        zin = zz[:, 0:2 * GT, :]
        zT = zz[:, 2 * GT:4 * GT, :]
        zflat = zz[:, :, :].rearrange("p t d -> p (t d)")[:, 0:WIDE]
        tb = sb("tb", [P, GT, D])
        t = sb("t", [P, GT, D])
        stats = sb("stats", [P, GT, 6])
        mv = sb("mv", [P, GT, 2])
        sd = sb("sd", [P, GT])
        rstd = sb("rstd", [P, GT])
        w0 = sb("w0", [P, 4, D])
        wc = sb("wc", [P, D1])
        wlin = sb("wlin", [D1, D])
        bc = sb("bc", [D1, 1])
        w2 = sb("w2", [P, 2, D])
        w3 = sb("w3", [P, LAYERS * (HOPS + 1), D])
        rows = sb("rows", [P, len(ROWS), D])
        rows3 = sb("rows3", [P, 3, LAYERS, D])
        ident = sb("ident", [P, P])
        ones = sb("ones", [P, P])
        iota_i = sb("iota_i", [P, P], I32)
        iota = sb("iota", [P, P])
        ci = sb("ci", [P, CG], I32)
        cf = sb("cf", [P, CG])
        number = sb("number", [P, CG])
        chunk_col = sb("chunk_col", [P, CG])
        chunk_idx = sb("chunk_idx", [P, CG], I32)
        base_col = sb("base_col", [P, CG])

        flat = hcur[:, :, :].rearrange("p t d -> p (t d)")
        ge = flat[:, 0:CG * STEPS].rearrange("p (k s) -> p k s", k=CG)
        oflat = acc[:, :, :].rearrange("p t d -> p (t d)")
        step_f = oflat[:, 0:STEPS]
        step_i = oflat[:, 896:896 + STEPS].bitcast(I32)
        chunk_f = oflat[0:1, 1792:1792 + STEPS]
        chunk_i = oflat[0:1, 2688:2688 + STEPS].bitcast(I32)
        tile_f = oflat[0:1, 3584:3584 + STEPS]
        rflat = ring[:, :, :].rearrange("p r d -> p (r d)")
        dnat_i = rflat[:, 0:896].bitcast(I32).rearrange("p (k e) -> p k e", k=CG)
        snat_i = rflat[:, 896:1792].bitcast(I32).rearrange("p (k e) -> p k e", k=CG)
        wnat = rflat[:, 1792:2688].rearrange("p (k e) -> p k e", k=CG)
        dnat = rflat[:, 2688:3584].rearrange("p (k e) -> p k e", k=CG)
        snat = rflat[:, 3584:4480].rearrange("p (k e) -> p k e", k=CG)
        dstep = rflat[:, 4480:5376].rearrange("p (k e) -> p k e", k=CG)
        wstep = rflat[:, 5376:6272].rearrange("p (k e) -> p k e", k=CG)
        wraw = rflat[:, 6272:6784].rearrange("p (w d) -> p w d", w=4)
        mflat = matrix[:, :, :].rearrange("p s n -> p (s n)")
        (l_dst, l_dst2, l_src, l_wgt, l_one, l_col, l_idx0, l_tmp) = (mflat[:, i * LANE:(i + 1) * LANE] for i in range(8))
        l_idx = l_idx0.bitcast(I32)
        l_ci, l_si = l_tmp.bitcast(I32), mflat[:, 8 * LANE:9 * LANE].bitcast(I32)

        pstep = [pb(f"pstep{i}", [P, 512]) for i in range(2)]
        pwide = pb("pwide", [P, WIDE])
        pT = pwide[:, 0:2048]
        pO = pwide[:, 2048:3072]

        def names(text):
            return [sem(n) for n in text.split()]

        (in_edges, in_x, in_w, g_const, v_nat, pad_out, p_walk, v_walk, walk_dma, v_steps, p_tabs, v_tabs,
         v_chain, a_deg) = names(
            "in_edges in_x in_w g_const v_nat pad_out p_walk v_walk walk_dma v_steps p_tabs v_tabs v_chain a_deg")
        landed = [sem(f"landed{q}") for q in range(NQ)]
        idx_staged, pe_step, hot_ready, acc_done, scales_ready = names(
            "idx_staged pe_step hot_ready acc_done scales_ready")
        (z_ready, zt_ps, zt_ready, h64_ps, h64_ready, o_ps, post_done, tb_ready, tb_sent, tb_free,
         table_done, var_ready, sd_ready, out_done, credits) = names(
            "z_ready zt_ps zt_ready h64_ps h64_ready o_ps post_done tb_ready tb_sent tb_free "
            "table_done var_ready sd_ready out_done credits")
        v_group = sem("v_group")
        zeroed, lanes_in, p_flag, v_flag, lanes_ready, lane_staged, swept, sweep_ready, merge_ps, x_copied, kept = names(
            "zeroed lanes_in p_flag v_flag lanes_ready lane_staged swept sweep_ready merge_ps x_copied kept")
        v_same = sem("v_same")
        acc_merged = sem("acc_merged")
        scattered = [sem(f"scattered{q}") for q in range(QS)]
        arrived = [sem(f"arrived{q}") for q in range(2)]
        pool_go, pe_go, act_go, dve_go, sp_go = names("pool_go pe_go act_go dve_go sp_go")

        DEG = STEPS
        STEP0 = RING
        table_v = table.rearrange("(t p) d -> p t d", p=P)
        out_v = out[0:(TILES - 1) * P, :].rearrange("(t p) d -> p t d", p=P)

        class Way:
            def __init__(self, hybrid):
                self.hybrid = hybrid
                self.steps = WALK if hybrid else STEPS
                self.chunks = C0 if hybrid else CHUNKS

            def step(self, a):
                return a * self.steps + (STEP0 + DEG)

            def added(self, a):
                return a * (self.steps + 1) + (DEG + 2)

            def built(self, a):
                return a * (self.steps // SUB + 1) + (DEG // SUB + 1)

        def ways(eng, name, program_of):
            reg = eng.alloc_register(f"{name}_flag")
            eng.wait_ge(v_flag, 1)
            eng.load([reg], flag_i[0:1, 0:1])
            spread = eng.snap(reg, min_val=0, max_val=1)
            with eng.If(spread > 0):
                program_of(Way(True))
            with eng.Else():
                program_of(Way(False))

        def stages(eng, way, stage_of):
            for a in range(STAGES):
                stage_of(way, a, a, None)
            with eng.Fori(0, LAYERS) as layer:
                for k in range(HOPS):
                    stage_of(way, layer * HOPS + (STAGES + k), "hop" + str(k + 1), layer)

        def uses_h(kind):
            return kind in (0, 1, "hop1")

        block = ctx.enter_context(nc.Block())

        @block.sync
        def _(sp):
            d, s, w = A["dst"], A["src"], A["edge_weight"]
            sp.wait_ge(v_nat, 3)
            for nat, a in ((dnat_i, d), (snat_i, s), (wnat, w)):
                k6 = 6 * P
                sp.dma_start(nat[:, 0:6, :], a[0:k6 * P].rearrange("(k p e) -> p k e", p=P, e=P)).then_inc(in_edges, 16)
                sp.dma_start(nat[0:FULL - k6, 6, :], a[k6 * P:FULL * P].rearrange("(p e) -> p e", e=P)).then_inc(in_edges, 16)
                sp.dma_start(nat[FULL - k6:FULL - k6 + 1, 6, 0:REST],
                             a[FULL * P:E].rearrange("(p e) -> p e", p=1)).then_inc(in_edges, 16)
            sp.dma_start(xres[:, 0:TILES - 1, :],
                         A["x"][0:(TILES - 1) * P, :].rearrange("(t p) d -> p t d", p=P)).then_inc(in_x, 16)
            sp.dma_start(xres[0:LAST, TILES - 1, :], A["x"][(TILES - 1) * P:N, :]).then_inc(in_x, 16)
            sp.wait_ge(v_nat, 6)
            sp.dma_start(dst_pad.rearrange("(k p) e -> p k e", p=P), dnat).then_inc(pad_out, 16)
            sp.dma_start(wgt_pad.rearrange("(k p) e -> p k e", p=P), wnat).then_inc(pad_out, 16)
            sp.dma_start(src_pad.rearrange("(k p) e -> p k e", p=P), snat).then_inc(pad_out, 16)
            sp.dma_start(first_dst[:, :], d[EDGE0:EDGE0 + 1].rearrange("(p e) -> p e", p=1)).then_inc(lanes_in, 16)
            sp.wait_ge(pad_out, 48)
            for to, pad, by in ((l_dst, dst_pad, 0), (l_dst2, dst_pad, LAP), (l_src, src_pad, 0), (l_wgt, wgt_pad, 0)):
                flat_pad = pad.rearrange("c e -> (c e)")
                sp.dma_start(to, flat_pad[EDGE0 + by:EDGE0 + by + LANE * P].rearrange("(p t) -> p t", p=P)).then_inc(lanes_in, 16)
            sp.wait_ge(in_x, 32)
            sp.dma_start(table_v, xres[:, :, :]).then_inc(x_copied, 16)

            def whole(way):
                if way.hybrid:
                    sp.wait_ge(v_nat, 6)
                    for m in (counts, weights):
                        with sp.Fori(0, TILES) as s:
                            sp.dma_start(m[bass.ds(s * P, P), :], zflat).then_inc(zeroed, 16)

                def dense(way, a, kind, layer):
                    if way.hybrid:
                        m = weights if layer is not None else counts
                        mv_ = m.rearrange("(s p) n -> p s n", p=P)
                        if kind == 0:
                            for q in range(QS):
                                sp.wait_ge(scattered[q], LAP * 32)
                            sp.wait_ge(x_copied, 16)
                        else:
                            sp.wait_ge(table_done, a * (GROUPS * 16))
                            sp.sem_inc(sp_go, 1)

                        def load(s, slot):
                            sp.dma_start(matrix[:, slot, :], mv_[:, bass.ds(s, 1), :]).then_inc(arrived[slot], 16)
                            sp.dma_start(hrow[:, slot, :], table_v[:, bass.ds(s, 1), :]).then_inc(arrived[slot], 16)
                        load(0, 0)
                        load(1, 1)
                        with sp.Fori(0, SWEEP - 1) as it:
                            for s in (2, 3):
                                sp.wait_ge(swept, a * TILES + it * 2 + (s - 1))
                                sp.sem_inc(sp_go, 1)
                                load(it * 2 + s, s % 2)
                        sp.wait_ge(swept, a * TILES + (2 * SWEEP - 1))
                        sp.sem_inc(sp_go, 1)
                        load(2 * SWEEP, 0)

                    with sp.Fori(0, GROUPS) as g:
                        sp.wait_ge(tb_ready, a * GROUPS + g + 1)
                        sp.sem_inc(sp_go, 1)
                        sp.dma_start(table_v[:, bass.ds(g * GT, GT), :], tb[:, :, :]).then_inc(table_done, 16)
                        sp.wait_ge(table_done, (a * GROUPS + g + 1) * 16)
                        sp.sem_inc(tb_free, 1)
                    if kind == 4:
                        sp.dma_start(x_kept, xres[:, :, :]).then_inc(kept, 16)
                stages(sp, way, dense)
                total = STAGES + LAYERS * HOPS
                sp.wait_ge(tb_ready, total * GROUPS)
                sp.dma_start(xres[:, :, :], x_kept).then_inc(kept, 16)
                for g in range(GROUPS):
                    sp.wait_ge(tb_ready, total * GROUPS + g + 1)
                    lo, hi = g * GT, (g + 1) * GT
                    n = GT if hi < TILES else GT - 1
                    sp.dma_start(out_v[:, lo:lo + n, :], tb[:, 0:n, :]).then_inc(out_done, 16)
                    if n < GT:
                        sp.dma_start(out[(TILES - 1) * P:N, :], tb[0:LAST, GT - 1, :]).then_inc(out_done, 16)
                    sp.wait_ge(out_done, (g + 1) * 16 + 16 * (n < GT))
                    sp.sem_inc(tb_free, 1)
            ways(sp, "sp", whole)

        @block.gpsimd
        def _(pool):
            pool.iota(iota_i[:, :], pattern=[[1, P]], base=0, channel_multiplier=0).then_inc(g_const, 1)
            pool.iota(ci[:, :], pattern=[[P, CG]], base=0, channel_multiplier=1).then_inc(g_const, 1)
            pool.iota(step_i, pattern=[[1, STEPS]], base=0, channel_multiplier=0).then_inc(g_const, 1)
            pool.memset(ones[:, :], 1.0).then_inc(g_const, 1)
            pool.memset(ident[:, :], 0.0).then_inc(g_const, 1)
            pool.wait_ge(g_const, 5)
            pool.affine_select(out=ident[:, :], in_=ident[:, :], compare_op=ALU.not_equal, fill=1.0, base=0,
                               pattern=[[-1, P]], channel_multiplier=1).then_inc(g_const, 1)
            pool.wait_ge(pad_out, 48)
            pool.wait_ge(v_walk, 1)
            for k in range(CG):
                for rows_, pad in ((dstep, dst_pad), (wstep, wgt_pad)):
                    pool.indirect_dma_start(out=rows_[:, k, :], out_offset=None, in_=pad[:, :],
                                            in_offset=bass.IndirectOffsetOnAxis(ap=chunk_idx[:, k:k + 1], axis=0)
                                            ).then_inc(walk_dma, 16)

            def scatter(rounds, before):
                for par in range(2):
                    pool.wait_ge(lane_staged, rounds * 2 + (par + 1))
                    for q in range(QS):
                        if before or par:
                            pool.wait_ge(scattered[q], rounds * 64 + par * 32)
                            pool.wait_ge(scattered[(q + 1) % QS], rounds * 64 + par * 32)
                        pool.sem_inc(pool_go, 1)
                        for m, value in ((counts, lane_1), (weights, lane_w)):
                            pool.indirect_dma_start(
                                out=m.rearrange("s (n a) -> (s n) a", a=1),
                                out_offset=bass.IndirectOffsetOnAxis(ap=lane_i[:, par, q:q + 1], axis=0),
                                in_=value[:, par, q:q + 1], in_offset=None, compute_op=ALU.add).then_inc(scattered[q], 16)

            def whole(way):
                if way.hybrid:
                    pool.wait_ge(zeroed, 2 * TILES * 16)
                    scatter(0, False)
                    with pool.Fori(1, LAP // 2) as r:
                        scatter(r, True)
                stages(pool, way, gather)

            def gather(way, a, kind, layer):
                if kind == 0:
                    pool.wait_ge(v_tabs, 1)
                    pool.wait_ge(x_copied, 16)
                else:
                    pool.wait_ge(table_done, a * (GROUPS * 16))
                    pool.sem_inc(pool_go, 1)

                def lap(it, n):
                    for s in range(0, n, SUB):
                        pool.wait_ge(pe_step, way.step(a) + it * RING + (s + SUB - NQ))
                        if s % NQ == 0:
                            pool.wait_ge(idx_staged, a * (way.chunks // NQ) + it * (RING // NQ) + (s // NQ + 1))
                        pool.sem_inc(pool_go, 1)
                        for c in range(s, s + SUB):
                            pool.indirect_dma_start(out=ring[:, c, :], out_offset=None, in_=table[:, :],
                                                    in_offset=bass.IndirectOffsetOnAxis(ap=stage[:, c:c + 1], axis=0)
                                                    ).then_inc(landed[c % NQ], 16)
                laps, rest = divmod(way.chunks, RING)
                with pool.Fori(0, laps) as it:
                    lap(it, RING)
                if rest:
                    lap(laps, rest)
            ways(pool, "pool", whole)

        @block.scalar
        def _(act):
            for i, n in enumerate(SQUARE):
                act.dma_start(wraw[:, i, :], A[n]).then_inc(in_w, 16)
            act.dma_start(wc[:, :], A["L1_gnn_W_conv"]).then_inc(in_w, 16)
            act.dma_start(wlin[:, :], A["L1_gnn_W_lin"]).then_inc(in_w, 16)
            act.dma_start(bc[:, :], A["L1_gnn_b_conv"].rearrange("(n a) -> n a", a=1)).then_inc(in_w, 16)
            act.dma_start(w2[:, 0, :], A["L2_gnn_W1"]).then_inc(in_w, 16)
            act.dma_start(w2[:, 1, :], A["L2_gnn_W2"]).then_inc(in_w, 16)
            act.dma_start(w3[:, :, :], A["L3_gnn_W"].rearrange("l k i o -> i (l k) o")).then_inc(in_w, 16)
            for i, n in enumerate(ROWS):
                act.dma_start(rows[:, i, :], A[n].partition_broadcast(P)).then_inc(in_w, 16)
            for i, n in enumerate(("bias", "gamma", "beta")):
                act.dma_start(rows3[:, i, :, :], A["L3_gnn_" + n].partition_broadcast(P)).then_inc(in_w, 16)

            def whole(way):
                if way.hybrid:
                    act.wait_ge(lanes_ready, 1)
                    halves = l_idx.bitcast(mybir.dt.uint16).rearrange("p (q r b) -> p r q b", r=LAP, b=2)
                    ones_v = l_one.rearrange("p (q r) -> p r q", r=LAP)
                    wgt_v = l_wgt.rearrange("p (q r) -> p r q", r=LAP)

                    def stage_round(r, par, before):
                        if before:
                            for q in range(QS):
                                act.wait_ge(scattered[q], r * 64 + (par - 1) * 32)
                            act.sem_inc(act_go, 1)
                        one = bass.ds(r * 2 + par, 1)
                        act.activation(lane_i[:, par:par + 1, :].bitcast(mybir.dt.uint16).rearrange("p a (q b) -> p a q b", b=2), halves[:, one, :, :], ACT.Copy)
                        act.activation(lane_w[:, par:par + 1, :], wgt_v[:, one, :], ACT.Copy)
                        act.activation(lane_1[:, par:par + 1, :], ones_v[:, one, :], ACT.Copy).then_inc(lane_staged, 1)
                    stage_round(0, 0, False)
                    stage_round(0, 1, False)
                    stage_round(1, 0, True)
                    stage_round(1, 1, True)
                    with act.Fori(2, LAP // 2) as r:
                        stage_round(r, 0, True)
                        stage_round(r, 1, True)
                act.wait_ge(v_steps, 2)
                act.activation(dtmp[:, :, :], dtmp[:, :, :], ACT.Sqrt).then_inc(a_deg, 1)
                stages(act, way, dense)
                with act.Fori(0, GROUPS) as g:
                    root(act, g + (3 + LAYERS) * GROUPS)

            def dense(way, a, kind, layer):
                if kind == 0:
                    act.wait_ge(v_tabs, 1)

                def quarter(it, q):
                    act.wait_ge(pe_step, way.step(a) + it * RING + ((q + 1) * NQ - RING))
                    act.sem_inc(act_go, 1)
                    act.activation(stage[:, q * NQ:(q + 1) * NQ], src_idx[:, bass.ds(it * RING + q * NQ, NQ)],
                                   ACT.Copy).then_inc(idx_staged, 1)
                laps, rest = divmod(way.chunks, RING)
                with act.Fori(0, laps) as it:
                    for q in range(RING // NQ):
                        quarter(it, q)
                for q in range(rest // NQ):
                    quarter(laps, q)
                if way.hybrid:
                    act.wait_ge(swept, a * TILES + TILES)
                    act.sem_inc(act_go, 1)
                    for b in range(0, WIDE, 512):
                        last = act.activation(zflat[:, b:b + 512], pwide[:, b:b + 512], ACT.Copy)
                    last.then_inc(sweep_ready, 1)
                n = 2 * GT if uses_h(kind) else GT
                with act.Fori(0, GROUPS) as g:
                    act.wait_ge(zt_ps, a * GROUPS + g + 1)
                    act.sem_inc(act_go, 1)
                    for lo in range(0, n, 4):
                        hi = min(lo + 4, n)
                        last = act.activation(zT[:, lo:hi, :].rearrange("p t n -> p (t n)"),
                                              pT[:, lo * P:hi * P], ACT.Copy)
                    last.then_inc(zt_ready, 1)
                    if kind == 2:
                        act.wait_ge(h64_ps, g + 1)
                        act.sem_inc(act_go, 1)
                        for lo, hi in ((0, 4), (4, 7)):
                            last = act.activation(zT[0:D1, GT + lo:GT + hi, :].rearrange("p t n -> p (t n)"),
                                                  pT[0:D1, lo * P:hi * P], ACT.Relu, bias=bc[:, :])
                        last.then_inc(h64_ready, 1)
                    norm = {1: 0, 2: 1, 4: 2}.get(kind)
                    if norm is not None:
                        root(act, norm * GROUPS + g)
                    if kind == "hop3":
                        root(act, (layer + 3) * GROUPS + g)

            def root(act, n):
                act.wait_ge(var_ready, n + 1)
                act.sem_inc(act_go, 1)
                act.activation(sd[:, :], sd[:, :], ACT.Sqrt).then_inc(sd_ready, 1)
            ways(act, "act", whole)

        @block.tensor
        def _(pe):
            pe.wait_ge(g_const, 6)
            pe.wait_ge(p_walk, 1)
            for half in range(2):
                for k in range(CG):
                    pe.matmul(pT[:, half * 512:half * 512 + STEPS // 2], ones[:, :],
                              ge[:, k, half * (STEPS // 2):(half + 1) * (STEPS // 2)], start=(k == 0), stop=(k == CG - 1))
            for s in range(CG):
                n = min(P, STEPS - s * P)
                for k in range(CG):
                    last = pe.matmul(pT[0:n, 1024 + s:1025 + s], ge[:, k, s * P:s * P + n], ones[:, 0:1],
                                     start=(k == 0), stop=(k == CG - 1))
            last.then_inc(p_tabs, 1)
            pe.wait_ge(v_nat, 6)
            for k in range(CG):
                last = pe.transpose(pO[:, k * P:(k + 1) * P], snat[:, k, :], ident[:, :])
            last.then_inc(p_tabs, 1)
            pe.wait_ge(in_w, 16 * (10 + len(ROWS) + 3))
            for i in range(4):
                last = pe.transpose(pstep[0][:, i * P:(i + 1) * P], wraw[:, i, :], ident[:, :])
            last.then_inc(p_tabs, 1)
            pe.wait_ge(v_same, 1)
            pe.matmul(pstep[1][0:1, 0:1], same[:, :], ones[:, 0:1], start=True, stop=True).then_inc(p_flag, 1)
            pe.wait_ge(v_walk, 2)
            for k in range(CG):
                last = pe.transpose(pT[:, k * P:(k + 1) * P], dstep[:, k, :], ident[:, :])
            last.then_inc(p_tabs, 1)
            for k in range(CG):
                last = pe.transpose(pT[:, 1024 + k * P:1024 + (k + 1) * P], wstep[:, k, :], ident[:, :])
            last.then_inc(p_tabs, 1)
            pe.sem_inc(pe_step, STEP0)
            slots = [pe.alloc_register(f"pe_slot{j}") for j in range(2 * SUB)]
            pe.wait_ge(v_tabs, 1)
            with pe.Fori(0, STEPS // (2 * SUB)) as it:
                for h in range(2):
                    pe.wait_ge(hot_ready, it * 2 + (h + 1))
                    pe.sem_inc(pe_go, 1)
                    for j in range(SUB):
                        pe.wait_ge(acc_done, it * (2 * SUB) + (h * SUB + j + 1))
                        pe.matmul(pstep[j % 2][:, 0:1], hot[:, h * SUB + j, :], ones[:, 0:1], start=True, stop=True)
                        pe.matmul(pstep[j % 2][:, 1:2], hot[:, h * SUB + j, :],
                                  wgt[:, bass.ds(it * (2 * SUB) + (h * SUB + j), 1)], start=True, stop=True
                                  ).then_inc(pe_step, 1)

            def step(way, a, it, j, gathers):
                if j % SUB == 0:
                    pe.wait_ge(hot_ready, way.built(a) + it * 2 + (j // SUB + 1))
                if gathers:
                    pe.wait_ge(landed[j], (a * (way.chunks // NQ) + it + 1) * 16)
                pe.wait_ge(acc_done, way.added(a) + it * (2 * SUB) + j)
                pe.sem_inc(pe_go, 1)
                slot = pe.snap(slots[j], min_val=0, max_val=RING - 1)
                pe.matmul(pstep[j % 2][:, 0:D], hot[:, j, :], ring[:, bass.ds(slot, 1), :],
                          start=True, stop=True).then_inc(pe_step, 1)

            def load_slots(it):
                for q in range(0, 2 * SUB, 4):
                    pe.load(slots[q:q + 4], slot_row[0:1, bass.ds(it * (2 * SUB) + q, 4)])

            def walk(way, a, gathers, lo, hi):
                with pe.Fori(lo, hi) as it:
                    load_slots(it)
                    for j in range(2 * SUB):
                        step(way, a, it, j, gathers)

            def both(way, a, it, last):
                load_slots(it)
                done = 0
                for m in range(12):
                    b = m % 6
                    if b == 0:
                        slot = 1 - m // 6
                        times = a * SWEEP + it + 1 if slot else a * (SWEEP + 1) + it + 2
                        pe.wait_ge(arrived[slot], times * 32)
                        pe.sem_inc(pe_go, 1)
                    mm = pe.matmul(pwide[:, b * 512:(b + 1) * 512], hrow[:, slot, :],
                                   matrix[:, slot, b * 512:(b + 1) * 512], start=False, stop=last and m >= 6)
                    if b == 5:
                        mm.then_inc(swept, 1)
                    while done < (m + 1) * 16 // 12:
                        step(way, a, it, done, True)
                        done += 1

            def dense(way, a, kind, layer):
                if way.hybrid:
                    pe.wait_ge(post_done, a * GROUPS + 1)
                    pe.wait_ge(arrived[0], (a * (SWEEP + 1) + 1) * 32)
                    pe.sem_inc(pe_go, 1)
                    for b in range(6):
                        mm = pe.matmul(pwide[:, b * 512:(b + 1) * 512], hrow[:, 0, :],
                                       matrix[:, 0, b * 512:(b + 1) * 512], start=True, stop=False)
                    mm.then_inc(swept, 1)
                    with pe.Fori(0, SWEEP - 1) as it:
                        both(way, a, it, False)
                    both(way, a, SWEEP - 1, True)
                    walk(way, a, True, SWEEP, C0 // NQ)
                    pe.wait_ge(sweep_ready, a + 1)
                    pe.sem_inc(pe_go, 1)
                    for j in range(TILES - T0):
                        mm = pe.transpose(pwide[:, j * P:(j + 1) * P], zflat[:, j * P:(j + 1) * P], ident[:, :])
                    mm.then_inc(merge_ps, 1)
                    walk(way, a, False, C0 // NQ, WALK // NQ)
                else:
                    walk(way, a, True, 0, CHUNKS // NQ)
                    walk(way, a, False, CHUNKS // NQ, STEPS // NQ)
                n = 2 * GT if uses_h(kind) else GT
                with pe.Fori(0, GROUPS) as g:
                    pe.wait_ge(z_ready, a * GROUPS + g + 1)
                    pe.sem_inc(pe_go, 1)
                    for j in range(n):
                        last = pe.transpose(pT[:, j * P:(j + 1) * P], zin[:, j, :], ident[:, :])
                    last.then_inc(zt_ps, 1)
                    pe.wait_ge(zt_ready, a * GROUPS + g + 1)
                    pe.wait_ge(post_done, a * GROUPS + g + 1)
                    pe.sem_inc(pe_go, 1)
                    if kind == 2:
                        zf = zT[:, 0:GT, :].rearrange("p t n -> p (t n)")
                        for lo, hi in ((0, 512), (512, GT * P)):
                            last = pe.matmul(pT[0:D1, lo:hi], wc[:, :], zf[:, lo:hi], start=True, stop=True)
                        last.then_inc(h64_ps, 1)
                        pe.wait_ge(h64_ready, g + 1)
                        pe.sem_inc(pe_go, 1)
                    for j in range(GT):
                        o = pO[:, j * P:(j + 1) * P]
                        z, h = zT[:, j, :], zT[:, GT + j, :]
                        if kind in (0, 1):
                            last = pe.matmul(o, z, w0[:, 2 * kind, :], start=True, stop=False)
                            last = pe.matmul(o, h, w0[:, 2 * kind + 1, :], start=False, stop=True)
                        elif kind == 2:
                            last = pe.matmul(o, zT[0:D1, GT + j, :], wlin[:, :], start=True, stop=True)
                        elif kind in (3, 4):
                            last = pe.matmul(o, z, w2[:, kind - 3, :], start=True, stop=True)
                        else:
                            k = int(kind[3])
                            if k == 1:
                                pe.matmul(o, h, w3[:, bass.ds(layer * (HOPS + 1), 1), :], start=True, stop=False)
                            last = pe.matmul(o, z, w3[:, bass.ds(layer * (HOPS + 1) + k, 1), :],
                                             start=(k != 1), stop=True)
                    last.then_inc(o_ps, 1)
            ways(pe, "pe", lambda way: stages(pe, way, dense))

        @block.vector
        def _(dve):
            V = nc.vector
            count = [0]

            def link(ins):
                count[0] += 1
                ins.then_inc(v_chain, 1)
                dve.wait_ge(v_chain, count[0])

            V.memset(xres[:, TILES - 1, :], 0.0)
            V.memset(dnat_i, PAD_DST).then_inc(v_nat, 1)
            V.memset(snat_i, 0).then_inc(v_nat, 1)
            V.memset(wnat, 0.0).then_inc(v_nat, 1)
            V.memset(zflat, 0.0).then_inc(v_nat, 1)
            V.memset(chunk_idx[:, :], 0)
            dve.sem_inc(post_done, 1)
            dve.sem_inc(tb_free, 1)
            dve.sem_inc(acc_done, 1)
            link(V.memset(chunk_col[:, :], 1.0))
            dve.wait_ge(in_edges, 144)
            V.tensor_copy(dnat, dnat_i).then_inc(v_nat, 1)
            V.tensor_copy(snat, snat_i).then_inc(v_nat, 1)
            dve.wait_ge(g_const, 6)
            V.tensor_copy(iota[:, :], iota_i[:, :])
            V.tensor_copy(step_f, step_i)
            link(V.tensor_copy(number[:, :], ci[:, :]))
            link(V.tensor_single_scalar(ci[:, :], dnat_i[:, :, 0], 7, ALU.arith_shift_right))
            link(V.tensor_copy(base_col[:, :], ci[:, :]))
            link(V.memset(base_col[0:1, 0:1], 0.0))
            link(V.tensor_scalar(base_col[:, :], base_col[:, :], float(TILES - 1), None, ALU.min))
            link(V.tensor_tensor(cf[:, :], number[:, :], base_col[:, :], ALU.add))
            for k in range(CG):
                last = V.tensor_scalar(ge[:, k, :], step_f, cf[:, k:k + 1], None, ALU.is_ge)
            last.then_inc(p_walk, 1)
            dve.wait_ge(p_tabs, 1)
            half = STEPS // 2
            for s in range(2):
                V.tensor_scalar(chunk_f[:, s * half:(s + 1) * half], pT[0:1, s * 512:s * 512 + half], -1.0, None, ALU.add)
            V.tensor_copy(chunk_col[:, 0:CG - 1], pT[:, 1024:1024 + CG - 1])
            tail = STEPS - (CG - 1) * P
            link(V.tensor_copy(chunk_col[0:tail, CG - 1:CG], pT[0:tail, 1024 + CG - 1:1024 + CG]))
            link(V.tensor_scalar(chunk_col[:, :], chunk_col[:, :], -1.0, None, ALU.add))
            V.tensor_copy(chunk_idx[:, :], chunk_col[:, :]).then_inc(v_walk, 1)
            link(V.tensor_tensor(tile_f, step_f[0:1, :], chunk_f, ALU.subtract))
            V.tensor_copy(tile_row[:, 0:STEPS], tile_f)
            link(V.tensor_copy(chunk_i, chunk_f))
            V.tensor_single_scalar(slot_row[:, 0:STEPS], chunk_i, RING - 1, ALU.bitwise_and)
            h = min(half, WALK)
            V.tensor_scalar(tail_mask[:, 0:h - C0], pT[:, C0:h], C0 + 0.5, 1e6, ALU.is_gt, ALU.mult)
            link(V.tensor_scalar(tail_mask[:, h - C0:WALK - C0], pT[:, 512:512 + WALK - h], C0 + 0.5, 1e6, ALU.is_gt, ALU.mult))
            dve.wait_ge(lanes_in, 80)
            link(V.tensor_scalar(l_one, l_dst, float(N), None, ALU.is_lt))
            link(V.tensor_tensor(l_dst2, l_dst, l_dst2, ALU.is_equal))
            link(V.tensor_tensor(l_dst2, l_dst2, l_one, ALU.mult))
            V.reduce_sum(same[:, :], l_dst2, axis=mybir.AxisListType.X).then_inc(v_same, 1)
            dve.wait_ge(v_same, 1)
            link(V.tensor_scalar(l_dst, l_dst, float(-T0 * P), None, ALU.add))
            link(V.tensor_tensor(l_dst, l_dst, step_f[:, 0:LANE], ALU.subtract))
            link(V.tensor_tensor(l_dst, l_dst, l_one, ALU.mult))
            link(V.tensor_tensor(l_dst, l_dst, step_f[:, 0:LANE], ALU.add))
            link(V.tensor_scalar(l_src, l_src, float(-PAD_SRC), None, ALU.add))
            link(V.tensor_tensor(l_src, l_src, l_one, ALU.mult))
            link(V.tensor_scalar(l_src, l_src, float(PAD_SRC), float(WIDE), ALU.add, ALU.mult))
            link(V.tensor_copy(l_ci, l_dst))
            link(V.tensor_copy(l_si, l_src))
            link(V.tensor_tensor(l_idx, l_ci, l_si, ALU.add))
            dve.sem_inc(lanes_ready, 1)
            dve.wait_ge(p_flag, 1)
            link(V.tensor_copy(flag[:, 0:1], first_dst[:, :]))
            link(V.tensor_scalar(flag[:, 1:2], flag[:, 0:1], float(T0 * P), None, ALU.is_ge))
            link(V.tensor_scalar(flag[:, 2:3], flag[:, 0:1], float((TEND + 1) * P), None, ALU.is_lt))
            link(V.tensor_scalar(flag[:, 3:4], pstep[1][0:1, 0:1], 0.5, None, ALU.is_lt))
            link(V.tensor_tensor(flag[:, 1:2], flag[:, 1:2], flag[:, 2:3], ALU.mult))
            link(V.tensor_tensor(flag[:, 1:2], flag[:, 1:2], flag[:, 3:4], ALU.mult))
            link(V.memset(flag_i[:, :], 0))
            link(V.tensor_copy(flag_i[:, 0:1], flag[:, 1:2]))
            dve.sem_inc(v_flag, 1)
            link(V.tensor_tensor(base_col[:, :], number[:, :], chunk_col[:, :], ALU.subtract))
            link(V.tensor_scalar(base_col[:, :], base_col[:, :], float(P), None, ALU.mult))
            dve.wait_ge(walk_dma, 16 * 2 * CG)
            for k in range(CG):
                last = V.tensor_scalar(dstep[:, k, :], dstep[:, k, :], base_col[:, k:k + 1], None, ALU.subtract)
            last.then_inc(v_walk, 1)
            dve.wait_ge(p_tabs, 2)
            V.tensor_copy(src_idx[:, :], pO[:, 0:CG * P])
            dve.wait_ge(p_tabs, 3)
            V.tensor_copy(w0[:, :, :].rearrange("p w d -> p (w d)"), pstep[0][:, :])
            dve.wait_ge(p_tabs, 5)
            V.tensor_copy(dst_rel[:, :], pT[:, 0:CG * P])
            link(V.tensor_copy(wgt[:, :], pT[:, 1024:1024 + CG * P]))
            dve.wait_ge(in_x, 32)
            dve.sem_inc(v_tabs, 1)
            tiles = [dve.alloc_register(f"dve_tile{j}") for j in range(SUB)]

            def build(it, h, weighted):
                for j in range(SUB):
                    i = it * (2 * SUB) + (h * SUB + j)
                    if weighted:
                        last = V.tensor_scalar(hot[:, h * SUB + j, :], iota[:, :], dst_rel[:, bass.ds(i, 1)],
                                               wgt[:, bass.ds(i, 1)], ALU.is_equal, ALU.mult)
                    else:
                        last = V.tensor_scalar(hot[:, h * SUB + j, :], iota[:, :], dst_rel[:, bass.ds(i, 1)],
                                               None, ALU.is_equal)
                last.then_inc(hot_ready, 1)

            def add(stepped, added, it, h, to_all, width):
                for q in (0, 4):
                    dve.load(tiles[q:q + 4], tile_row[0:1, bass.ds(it * (2 * SUB) + (h * SUB + q), 4)])
                for j in range(SUB):
                    tile = dve.snap(tiles[j], min_val=0, max_val=TILES - 1)
                    i = it * (2 * SUB) + (h * SUB + j)
                    dve.wait_ge(pe_step, stepped + i + 1)
                    dve.wait_ge(acc_done, added + i + 1)
                    to = to_all[:, bass.ds(tile, 1), :]
                    V.tensor_tensor(to, to, pstep[j % 2][:, 0:width].rearrange("p (a d) -> p a d", a=1),
                                    ALU.add).then_inc(acc_done, 1)

            def walk(stepped, added, steps, weighted, to_all, width):
                build(0, 0, weighted)
                with dve.Fori(0, steps // (2 * SUB)) as it:
                    build(it, 1, weighted)
                    add(stepped, added, it, 0, to_all, width)
                    build(it + 1, 0, weighted)
                    add(stepped, added, it, 1, to_all, width)
                dve.wait_ge(acc_done, added + (steps + 1))
                dve.sem_inc(dve_go, 1)

            V.memset(degs[:, :, :], 0.0).then_inc(acc_done, 1)
            walk(STEP0, 1, STEPS, False, degs, 2)

            def degrees():
                link(V.tensor_scalar(rcnt[:, :], degs[:, :, 0], 1.0, None, ALU.max))
                link(V.reciprocal(rcnt[:, :], rcnt[:, :]))
                link(V.tensor_scalar(degs[:, :, 0], degs[:, :, 0], 1.0, None, ALU.add))
                d2 = degs[:, :, :].rearrange("p t c -> p c t")
                link(V.tensor_scalar(dmask[:, :, :], d2, 0.0, None, ALU.is_gt))
                link(V.tensor_scalar(dinv[:, :, :], dmask[:, :, :], -1.0, 1.0, ALU.mult, ALU.add))
                link(V.tensor_tensor(dtmp[:, :, :], d2, dmask[:, :, :], ALU.mult))
                link(V.tensor_tensor(dtmp[:, :, :], dtmp[:, :, :], dinv[:, :, :], ALU.add))
                dve.sem_inc(v_steps, 2)
                dve.wait_ge(a_deg, 1)
                link(V.reciprocal(dinv[:, :, :], dtmp[:, :, :]))
                link(V.tensor_tensor(dinv[:, :, :], dinv[:, :, :], dmask[:, :, :], ALU.mult))

            def wide(col):
                return col.broadcast_to([P, GT, D])

            def column(x):
                return x.rearrange("p (t a) -> p t a", a=1)

            degrees()

            def whole(way):
                if way.hybrid:
                    link(V.tensor_tensor(dst_rel[:, C0:WALK], dst_rel[:, C0:WALK], tail_mask[:, :], ALU.add))
                stages(dve, way, dense)
                final()

            def dense(way, a, kind, layer):
                if kind in (2, 3, 4):
                    dve.sem_inc(acc_done, 1)
                else:
                    V.memset(acc[:, :, :], 0.0).then_inc(acc_done, 1)
                walk(way.step(a), way.added(a), way.steps, layer is not None, acc, D)
                if way.hybrid:
                    dve.wait_ge(merge_ps, a + 1)
                    dve.sem_inc(dve_go, 1)
                    V.tensor_tensor(acc[:, T0:TILES, :], acc[:, T0:TILES, :],
                                    pwide[:, :].rearrange("p (t d) -> p t d", d=D), ALU.add).then_inc(acc_merged, 1)
                    dve.wait_ge(acc_merged, a + 1)
                    dve.sem_inc(dve_go, 1)
                if kind == "hop1":
                    dve.wait_ge(kept, 16)
                scale = rcnt[:, :] if kind in (0, 1) else dinv[:, 0, :] if kind in (2, 3, 4) else dinv[:, 1, :]
                after = None if kind in (0,) else dinv[:, 0, :] if kind in (1, 2, 3) else dinv[:, 1, :]
                start = [0]
                with dve.Fori(0, GROUPS) as g:
                    G = a * GROUPS + g

                    def chained(ins):
                        start[0] += 1
                        ins.then_inc(v_group, 1)
                        dve.wait_ge(v_group, G * LINKS + start[0])
                        dve.sem_inc(dve_go, 1)
                    sl = bass.ds(g * GT, GT)
                    ins = V.tensor_tensor(zin[:, 0:GT, :], acc[:, sl, :], wide(column(scale[:, sl])), ALU.mult)
                    if uses_h(kind):
                        ins = V.tensor_copy(zin[:, GT:2 * GT, :], (xres if kind == 0 else hcur)[:, sl, :])
                    chained(ins)
                    dve.sem_inc(z_ready, 1)
                    if kind in ("hop1", "hop2"):
                        dve.wait_ge(tb_free, G + 1)
                        dve.sem_inc(dve_go, 1)
                        V.tensor_tensor(tb[:, :, :], zin[:, 0:GT, :], wide(column(after[:, sl])), ALU.mult).then_inc(tb_ready, 1)
                    dve.wait_ge(o_ps, G + 1)
                    dve.sem_inc(dve_go, 1)
                    po = pO[:, 0:GT * P].rearrange("p (t d) -> p t d", t=GT)
                    if kind == "hop1":
                        V.tensor_copy(outacc[:, sl, :], po).then_inc(post_done, 1)
                    elif kind == "hop2":
                        V.tensor_tensor(outacc[:, sl, :], outacc[:, sl, :], po, ALU.add).then_inc(post_done, 1)
                    else:
                        if layer is None:
                            row = rows[:, kind:kind + 1, :]
                        else:
                            row = rows3[:, 0, bass.ds(layer, 1), :]
                        chained(V.tensor_tensor(t[:, :, :], po, row.broadcast_to([P, GT, D]), ALU.add))
                        dve.sem_inc(post_done, 1)
                        if kind in (0, 3):
                            chained(V.tensor_scalar(hcur[:, sl, :], t[:, :, :], 0.0, None, ALU.max))
                            new = hcur
                        else:
                            if kind == "hop3":
                                chained(V.tensor_tensor(t[:, :, :], t[:, :, :], outacc[:, sl, :], ALU.add))
                                res = hcur
                            else:
                                res = xres
                            chained(V.tensor_tensor(t[:, :, :], t[:, :, :], res[:, sl, :], ALU.add))
                            ln = {1: 0, 2: 1, 4: 2}.get(kind)
                            n = ln * GROUPS + g if ln is not None else (layer + 3) * GROUPS + g
                            normalise(n, chained)
                            if kind == "hop3":
                                chained(V.tensor_tensor(t[:, :, :], t[:, :, :],
                                                        rows3[:, 1, bass.ds(layer, 1), :].broadcast_to([P, GT, D]), ALU.mult))
                                chained(V.tensor_tensor(t[:, :, :], t[:, :, :],
                                                        rows3[:, 2, bass.ds(layer, 1), :].broadcast_to([P, GT, D]), ALU.add))
                                chained(V.tensor_scalar(hcur[:, sl, :], t[:, :, :], 0.0, None, ALU.max))
                                new = hcur
                            else:
                                chained(V.tensor_copy(xres[:, sl, :], t[:, :, :]))
                                if kind == 4:
                                    chained(V.tensor_copy(hcur[:, sl, :], t[:, :, :]))
                                new = xres
                        dve.wait_ge(tb_free, G + 1)
                        dve.sem_inc(dve_go, 1)
                        if after is None:
                            V.tensor_copy(tb[:, :, :], new[:, sl, :]).then_inc(tb_ready, 1)
                        else:
                            if kind in (1, 2, 3):
                                chained(V.tensor_tensor(acc[:, sl, :], new[:, sl, :], wide(column(after[:, sl])), ALU.mult))
                            V.tensor_tensor(tb[:, :, :], new[:, sl, :], wide(column(after[:, sl])), ALU.mult).then_inc(tb_ready, 1)
                    dve.wait_ge(tb_ready, G + 1)
                    dve.wait_ge(post_done, G + 2)
                    dve.sem_inc(dve_go, 1)
                    dve.sem_inc(v_group, LINKS - start[0])
                assert start[0] < LINKS

            def normalise(n, chained):
                for j in range(GT):
                    ins = V.bn_stats(stats[:, j, :], t[:, j, :])
                chained(ins)
                for j in range(GT):
                    ins = V.bn_aggr(mv[:, j, :], stats[:, j, :])
                chained(ins)
                chained(V.tensor_scalar(sd[:, :], mv[:, :, 1], EPS, None, ALU.add))
                dve.sem_inc(var_ready, 1)
                dve.wait_ge(sd_ready, n + 1)
                dve.sem_inc(dve_go, 1)
                chained(V.reciprocal(rstd[:, :], sd[:, :]))
                for j in range(GT):
                    ins = V.tensor_scalar(t[:, j, :], t[:, j, :], mv[:, j, 0:1], rstd[:, j:j + 1], ALU.subtract, ALU.mult)
                chained(ins)

            def final():
                dve.wait_ge(kept, 32)
                start = [0]
                total = STAGES + LAYERS * HOPS
                with dve.Fori(0, GROUPS) as g:
                    G = g + total * GROUPS

                    def chained(ins):
                        start[0] += 1
                        ins.then_inc(v_group, 1)
                        dve.wait_ge(v_group, G * LINKS + start[0])
                        dve.sem_inc(dve_go, 1)
                    sl = bass.ds(g * GT, GT)
                    chained(V.tensor_tensor(t[:, :, :], xres[:, sl, :], hcur[:, sl, :], ALU.add))
                    normalise(g + (3 + LAYERS) * GROUPS, chained)
                    dve.wait_ge(tb_free, G + 1)
                    dve.sem_inc(dve_go, 1)
                    V.tensor_copy(tb[:, :, :], t[:, :, :]).then_inc(tb_ready, 1)
                    dve.wait_ge(tb_ready, G + 1)
                    dve.sem_inc(v_group, LINKS - start[0])

            ways(dve, "dve", whole)


_INS = ["x", "src", "dst", "edge_weight", "L0_gnn_W1l", "L0_gnn_b1l", "L0_gnn_W1r", "L0_gnn_W2l", "L0_gnn_b2l",
        "L0_gnn_W2r", "L1_gnn_W_conv", "L1_gnn_b_conv", "L1_gnn_W_lin", "L1_gnn_b_lin", "L2_gnn_W1", "L2_gnn_b1",
        "L2_gnn_W2", "L2_gnn_b2", "L3_gnn_W", "L3_gnn_bias", "L3_gnn_gamma", "L3_gnn_beta"]


def kernel(**inputs):
    import numpy as np
    import concourse.bacc as bacc
    from concourse.bass_utils import run_bass_kernel_spmd

    nc = bacc.Bacc("TRN2", target_bir_lowering=False, num_devices=1)
    arrays, A = {}, {}
    for name in _INS:
        a = np.ascontiguousarray(inputs[name])
        arrays[f"in_{name}"] = a
        A[name] = nc.dram_tensor(f"in_{name}", a.shape, mybir.dt.from_np(a.dtype), kind="ExternalInput").ap()
    out = nc.dram_tensor("out", (N, D), F32, kind="ExternalOutput").ap()
    program(nc, A, out)
    r = run_bass_kernel_spmd(nc, [arrays], core_ids=[0])
    return r.results[0]["out"]
```

```python
import concourse.bass as bass
from concourse import mybir
from contextlib import ExitStack

F32 = mybir.dt.float32
I32 = mybir.dt.int32
ALU = mybir.AluOpType
ACT = mybir.ActivationFunctionType

P = 128
N, D, E = 6250, 128, 106250
D1 = 64
TILES = -(-N // P)
LAST = N - (TILES - 1) * P
CHUNKS = 832
STEPS = CHUNKS + TILES - 1
CG = 7
FULL = E // P
REST = E - FULL * P
NQ = 16
AHEAD = 32
RING = 64
SUB = 8
BATCH = 4
BODY = 16
GT = 7
GROUPS = TILES // GT
PAD_DST = 1 << 20
EPS = 1e-5
HOPS = 3
LAYERS = 3
LINKS = 16
STAGES = 5
assert RING >= AHEAD + 32 and RING >= NQ + TILES - 1 and STEPS % BODY == 0
assert CHUNKS % RING == 0 and TILES % GT == 0

C0 = 432
T0 = 25
TEND = 31
WALK = C0 + TEND + 1
WIDE = (TILES - T0) * P
EDGE0 = C0 * P
LANE = (CHUNKS - C0) * P // P
QS = 8
LAP = LANE // QS
PAD_SRC = N + 10
LAGS = ((24, 16), (25, 20))
BIAS = 16
MERGE = 26
SWEEP = 24
assert WALK % BODY == 0 and C0 % NQ == 0 and LANE % QS == 0 and WIDE == 6 * 512
assert 2 * SWEEP + 1 == TILES and LAGS[0][0] == SWEEP and LAGS[1][0] == MERGE - 1

ROWS = ["L0_gnn_b1l", "L0_gnn_b2l", "L1_gnn_b_lin", "L2_gnn_b1", "L2_gnn_b2"]
SQUARE = ["L0_gnn_W1l", "L0_gnn_W1r", "L0_gnn_W2l", "L0_gnn_W2r"]


def program(nc, A, out):
    ctx = ExitStack()
    with ctx:
        def sb(name, shape, dt=F32):
            return ctx.enter_context(nc.sbuf_tensor(name, shape, dt))

        def pb(name, shape):
            return ctx.enter_context(nc.psum_tensor(name, shape, F32))

        def sem(name):
            return ctx.enter_context(nc.semaphore(name))

        table = nc.dram_tensor("table", (TILES * P, D), F32, kind="Internal").ap()
        dst_pad = nc.dram_tensor("dst_pad", (CG * P, P), F32, kind="Internal").ap()
        wgt_pad = nc.dram_tensor("wgt_pad", (CG * P, P), F32, kind="Internal").ap()
        src_pad = nc.dram_tensor("src_pad", (CG * P, P), F32, kind="Internal").ap()
        counts = nc.dram_tensor("counts", (TILES * P, WIDE), F32, kind="Internal").ap()
        weights = nc.dram_tensor("weights", (TILES * P, WIDE), F32, kind="Internal").ap()
        x_kept = nc.dram_tensor("x_kept", (TILES, P, D), F32, kind="Internal").ap().rearrange("t p d -> p t d")

        xres = sb("xres", [P, TILES, D])
        hcur = sb("hcur", [P, TILES, D])
        outacc = xres
        acc = sb("acc", [P, TILES, D])
        degs = sb("degs", [P, TILES, 2])
        rcnt = sb("rcnt", [P, TILES])
        dinv = sb("dinv", [P, 2, TILES])
        dtmp = sb("dtmp", [P, 2, TILES])
        dmask = sb("dmask", [P, 2, TILES])
        src_idx = sb("src_idx", [P, CG * P], I32)
        dst_rel = sb("dst_rel", [P, CG * P])
        wgt = sb("wgt", [P, CG * P])
        tail_mask = sb("tail_mask", [P, WALK - C0])
        flag = sb("flag", [1, 4])
        flag_i = sb("flag_i", [1, 4], I32)
        first_dst = sb("first_dst", [1, 1], I32)
        same = sb("same", [P, 1])
        matrix = sb("matrix", [P, 2, WIDE])
        hrow = sb("hrow", [P, 2, D])
        lane_i = sb("lane_i", [P, 2, QS], I32)
        lane_v = sb("lane_v", [P, 2, QS])
        slot_row = sb("slot_row", [1, CG * P], I32)
        tile_row = sb("tile_row", [1, CG * P], I32)
        ring = sb("ring", [P, RING, D])
        stage = sb("stage", [P, RING], I32)
        hot = sb("hot", [P, BODY, P])
        zz = sb("zz", [P, 4 * GT, D])
        zin = zz[:, 0:2 * GT, :]
        zT = zz[:, 2 * GT:4 * GT, :]
        zflat = zz[:, :, :].rearrange("p t d -> p (t d)")[:, 0:WIDE]
        tb = sb("tb", [P, GT, D])
        t = sb("t", [P, GT, D])
        stats = sb("stats", [P, GT, 6])
        mv = sb("mv", [P, GT, 2])
        sd = sb("sd", [P, GT])
        rstd = sb("rstd", [P, GT])
        w0 = sb("w0", [P, 4, D])
        wc = sb("wc", [P, D1])
        wlin = sb("wlin", [D1, D])
        bc = sb("bc", [D1, 1])
        w2 = sb("w2", [P, 2, D])
        w3 = sb("w3", [P, LAYERS * (HOPS + 1), D])
        rows = sb("rows", [P, len(ROWS), D])
        rows3 = sb("rows3", [P, 3, LAYERS, D])
        ident = sb("ident", [P, P])
        zero_col = sb("zero_col", [P, 1, 1])
        ones = sb("ones", [P, P])
        iota_i = sb("iota_i", [P, P], I32)
        iota = sb("iota", [P, P])
        ci = sb("ci", [P, CG], I32)
        cf = sb("cf", [P, CG])
        number = sb("number", [P, CG])
        chunk_col = sb("chunk_col", [P, CG])
        chunk_idx = sb("chunk_idx", [P, CG], I32)
        base_col = sb("base_col", [P, CG])

        flat = hcur[:, :, :].rearrange("p t d -> p (t d)")
        ge = flat[:, 0:CG * STEPS].rearrange("p (k s) -> p k s", k=CG)
        oflat = acc[:, :, :].rearrange("p t d -> p (t d)")
        step_f = oflat[:, 0:STEPS]
        step_i = oflat[:, 896:896 + STEPS].bitcast(I32)
        chunk_f = oflat[0:1, 1792:1792 + STEPS]
        chunk_i = oflat[0:1, 2688:2688 + STEPS].bitcast(I32)
        tile_f = oflat[0:1, 3584:3584 + STEPS]
        rflat = ring[:, :, :].rearrange("p r d -> p (r d)")
        dnat_i = rflat[:, 0:896].bitcast(I32).rearrange("p (k e) -> p k e", k=CG)
        snat_i = rflat[:, 896:1792].bitcast(I32).rearrange("p (k e) -> p k e", k=CG)
        wnat = rflat[:, 1792:2688].rearrange("p (k e) -> p k e", k=CG)
        dnat = rflat[:, 2688:3584].rearrange("p (k e) -> p k e", k=CG)
        snat = rflat[:, 3584:4480].rearrange("p (k e) -> p k e", k=CG)
        dstep = rflat[:, 4480:5376].rearrange("p (k e) -> p k e", k=CG)
        wstep = rflat[:, 5376:6272].rearrange("p (k e) -> p k e", k=CG)
        wraw = rflat[:, 6272:6784].rearrange("p (w d) -> p w d", w=4)
        mflat = matrix[:, :, :].rearrange("p s n -> p (s n)")
        (l_dst, l_dst2, l_src, l_wgt, l_one, l_idx0, l_tmp) = (mflat[:, i * LANE:(i + 1) * LANE] for i in range(7))
        l_idx = l_idx0.bitcast(I32)
        l_ci, l_si = l_tmp.bitcast(I32), mflat[:, 8 * LANE:9 * LANE].bitcast(I32)

        pstep = [pb(f"pstep{i}", [P, 512]) for i in range(2)]
        pwide = pb("pwide", [P, WIDE])
        pT = pwide[:, 0:2048]
        pO = pwide[:, 2048:3072]

        def names(text):
            return [sem(n) for n in text.split()]

        (in_edges, in_x, in_w, g_const, v_nat, pad_out, p_walk, v_walk, walk_dma, v_steps, p_tabs, v_tabs,
         v_chain, a_deg) = names(
            "in_edges in_x in_w g_const v_nat pad_out p_walk v_walk walk_dma v_steps p_tabs v_tabs v_chain a_deg")
        landed = [sem(f"landed{q}") for q in range(NQ)]
        idx_staged, pe_step, hot_ready, acc_done = names("idx_staged pe_step hot_ready acc_done")
        (z_ready, zt_ps, zt_ready, h64_ps, h64_ready, o_ps, post_done, tb_ready, tb_sent, tb_free,
         table_done, var_ready, sd_ready, out_done) = names(
            "z_ready zt_ps zt_ready h64_ps h64_ready o_ps post_done tb_ready tb_sent tb_free "
            "table_done var_ready sd_ready out_done")
        v_group = sem("v_group")
        lanes_in, p_flag, v_flag, lanes_ready, lane_staged, swept, sweep_ready, merge_ps, x_copied, kept = names(
            "lanes_in p_flag v_flag lanes_ready lane_staged swept sweep_ready merge_ps x_copied kept")
        zeroed_counts, zeroed_weights = ([sem(f"zeroed_{m}{i}") for i in range(2)] for m in ("counts", "weights"))
        back = [sem(f"back{g}") for g in range(GROUPS)]
        acc_final = sem("acc_final")
        v_same = sem("v_same")
        acc_merged = sem("acc_merged")
        scattered = [sem(f"scattered{q}") for q in range(QS)]
        arrived = [sem(f"arrived{q}") for q in range(2)]
        pool_go, pe_go, act_go, dve_go, sp_go = names("pool_go pe_go act_go dve_go sp_go")

        DEG = STEPS
        ACC0 = BATCH
        STEP0 = RING
        table_v = table.rearrange("(t p) d -> p t d", p=P)
        out_v = out[0:(TILES - 1) * P, :].rearrange("(t p) d -> p t d", p=P)

        class Way:
            def __init__(self, hybrid):
                self.hybrid = hybrid
                self.steps = WALK if hybrid else STEPS
                self.chunks = C0 if hybrid else CHUNKS

            def step(self, a):
                return a * self.steps + (STEP0 + DEG)

            def added(self, a):
                return a * (self.steps + 1) + (ACC0 + DEG + 1)

            def built(self, a):
                return a * (self.steps // BATCH + 2) + (DEG // BATCH + 2)

        def ways(eng, name, program_of):
            reg = eng.alloc_register(f"{name}_flag")
            eng.wait_ge(v_flag, 1)
            eng.load([reg], flag_i[0:1, 0:1])
            spread = eng.snap(reg, min_val=0, max_val=1)
            with eng.If(spread > 0):
                program_of(Way(True))
            with eng.Else():
                program_of(Way(False))

        def zero(eng, matrix_, zeroed, go):
            def one(s, par):
                eng.dma_start(matrix_[bass.ds(s * P, P), :], zflat).then_inc(zeroed[par], 16)
            one(0, 0)
            one(1, 1)
            with eng.Fori(1, TILES // 2) as it:
                for par in range(2):
                    eng.wait_ge(zeroed[par], it * 16)
                    eng.sem_inc(go, 1)
                    one(it * 2 + par, par)
            eng.wait_ge(zeroed[0], TILES // 2 * 16)
            one(TILES - 1, 0)

        def wait_zeroed(eng, zeroed):
            for par in range(2):
                eng.wait_ge(zeroed[par], (TILES + 1 - par) // 2 * 16)

        def stages(eng, way, stage_of):
            for a in range(STAGES):
                stage_of(way, a, a, None)
            with eng.Fori(0, LAYERS) as layer:
                for k in range(HOPS):
                    stage_of(way, layer * HOPS + (STAGES + k), "hop" + str(k + 1), layer)

        def scale_of(kind):
            return rcnt[:, :] if kind in (0, 1) else dinv[:, 0, :] if kind in (2, 3, 4) else dinv[:, 1, :]

        def uses_h(kind):
            return kind in (0, 1, "hop1")

        block = ctx.enter_context(nc.Block())

        @block.sync
        def _(sp):
            d, s, w = A["dst"], A["src"], A["edge_weight"]
            sp.wait_ge(v_nat, 3)
            for nat, a in ((dnat_i, d), (snat_i, s), (wnat, w)):
                k6 = 6 * P
                sp.dma_start(nat[:, 0:6, :], a[0:k6 * P].rearrange("(k p e) -> p k e", p=P, e=P)).then_inc(in_edges, 16)
                sp.dma_start(nat[0:FULL - k6, 6, :], a[k6 * P:FULL * P].rearrange("(p e) -> p e", e=P)).then_inc(in_edges, 16)
                sp.dma_start(nat[FULL - k6:FULL - k6 + 1, 6, 0:REST],
                             a[FULL * P:E].rearrange("(p e) -> p e", p=1)).then_inc(in_edges, 16)
            sp.dma_start(xres[:, 0:TILES - 1, :],
                         A["x"][0:(TILES - 1) * P, :].rearrange("(t p) d -> p t d", p=P)).then_inc(in_x, 16)
            sp.dma_start(xres[0:LAST, TILES - 1, :], A["x"][(TILES - 1) * P:N, :]).then_inc(in_x, 16)
            sp.wait_ge(v_nat, 6)
            sp.dma_start(dst_pad.rearrange("(k p) e -> p k e", p=P), dnat).then_inc(pad_out, 16)
            sp.dma_start(wgt_pad.rearrange("(k p) e -> p k e", p=P), wnat).then_inc(pad_out, 16)
            sp.dma_start(src_pad.rearrange("(k p) e -> p k e", p=P), snat).then_inc(pad_out, 16)
            sp.dma_start(first_dst[:, :], d[EDGE0:EDGE0 + 1].rearrange("(p e) -> p e", p=1)).then_inc(lanes_in, 16)
            sp.wait_ge(pad_out, 48)
            for to, pad, by in ((l_dst, dst_pad, 0), (l_dst2, dst_pad, LAP), (l_src, src_pad, 0), (l_wgt, wgt_pad, 0)):
                flat_pad = pad.rearrange("c e -> (c e)")
                sp.dma_start(to, flat_pad[EDGE0 + by:EDGE0 + by + LANE * P].rearrange("(p t) -> p t", p=P)).then_inc(lanes_in, 16)
            sp.wait_ge(in_x, 32)
            sp.dma_start(table_v, xres[:, :, :]).then_inc(x_copied, 16)
            wait_zeroed(sp, zeroed_counts)
            zero(sp, weights, zeroed_weights, sp_go)

            def whole(way):
                def dense(way, a, kind, layer):
                    if way.hybrid:
                        m = weights if layer is not None else counts
                        mv_ = m.rearrange("(s p) n -> p s n", p=P)
                        if kind == 0:
                            for q in range(QS):
                                sp.wait_ge(scattered[q], LAP * 32)
                            sp.wait_ge(x_copied, 16)
                        else:
                            sp.wait_ge(table_done, a * (GROUPS * 16))
                            sp.sem_inc(sp_go, 1)

                        def load(s, slot):
                            sp.dma_start(matrix[:, slot, :], mv_[:, bass.ds(s, 1), :]).then_inc(arrived[slot], 16)
                            sp.dma_start(hrow[:, slot, :], table_v[:, bass.ds(s, 1), :]).then_inc(arrived[slot], 16)
                        load(0, 0)
                        load(1, 1)
                        with sp.Fori(0, SWEEP - 1) as it:
                            for s in (2, 3):
                                sp.wait_ge(swept, a * TILES + it * 2 + (s - 1))
                                sp.sem_inc(sp_go, 1)
                                load(it * 2 + s, s % 2)
                        sp.wait_ge(swept, a * TILES + (2 * SWEEP - 1))
                        sp.sem_inc(sp_go, 1)
                        load(2 * SWEEP, 0)

                    rows_in = {0: hcur, 1: acc, 2: acc, 3: acc, "hop1": ring, "hop2": ring}.get(kind)
                    with sp.Fori(0, GROUPS) as g:
                        sp.wait_ge(tb_ready, a * GROUPS + g + 1)
                        sp.sem_inc(sp_go, 1)
                        from_ = tb[:, :, :] if rows_in is None else rows_in[:, bass.ds(g * GT, GT), :]
                        sp.dma_start(table_v[:, bass.ds(g * GT, GT), :], from_).then_inc(table_done, 16)
                        if rows_in is None:
                            sp.wait_ge(table_done, (a * GROUPS + g + 1) * 16)
                            sp.sem_inc(tb_free, 1)
                    if rows_in is not None:
                        sp.wait_ge(table_done, (a + 1) * (GROUPS * 16))
                        sp.sem_inc(tb_free, GROUPS)
                    if kind == 4:
                        sp.dma_start(x_kept, hcur[:, :, :]).then_inc(kept, 16)
                stages(sp, way, dense)
                total = STAGES + LAYERS * HOPS
                sp.wait_ge(tb_ready, total * GROUPS)
                for g in range(GROUPS):
                    sl = slice(g * GT, (g + 1) * GT)
                    sp.dma_start(xres[:, sl, :], x_kept[:, sl, :]).then_inc(back[g], 16)
                for g in range(GROUPS):
                    sp.wait_ge(tb_ready, total * GROUPS + g + 1)
                    lo, hi = g * GT, min((g + 1) * GT, TILES - 1)
                    sp.dma_start(out_v[:, lo:hi, :], acc[:, lo:hi, :]).then_inc(out_done, 16)
                sp.dma_start(out[(TILES - 1) * P:N, :], acc[0:LAST, TILES - 1, :]).then_inc(out_done, 16)
                sp.wait_ge(out_done, (GROUPS + 1) * 16)
            ways(sp, "sp", whole)

        @block.gpsimd
        def _(pool):
            pool.iota(iota_i[:, :], pattern=[[1, P]], base=0, channel_multiplier=0).then_inc(g_const, 1)
            pool.iota(ci[:, :], pattern=[[P, CG]], base=0, channel_multiplier=1).then_inc(g_const, 1)
            pool.iota(step_i, pattern=[[1, STEPS]], base=0, channel_multiplier=0).then_inc(g_const, 1)
            pool.memset(ones[:, :], 1.0).then_inc(g_const, 1)
            pool.memset(ident[:, :], 0.0).then_inc(g_const, 1)
            pool.wait_ge(g_const, 5)
            pool.affine_select(out=ident[:, :], in_=ident[:, :], compare_op=ALU.not_equal, fill=1.0, base=0,
                               pattern=[[-1, P]], channel_multiplier=1).then_inc(g_const, 1)
            pool.wait_ge(pad_out, 48)
            pool.wait_ge(v_walk, 1)
            for k in range(CG):
                for rows_, pad in ((dstep, dst_pad), (wstep, wgt_pad)):
                    pool.indirect_dma_start(out=rows_[:, k, :], out_offset=None, in_=pad[:, :],
                                            in_offset=bass.IndirectOffsetOnAxis(ap=chunk_idx[:, k:k + 1], axis=0)
                                            ).then_inc(walk_dma, 16)

            def scatter(which, m, rounds, first):
                for par in range(2):
                    before = which * LAP + rounds * 2 + par
                    pool.wait_ge(lane_staged, before + 1)
                    for q in range(QS):
                        if not first or par:
                            pool.wait_ge(scattered[q], before * 16)
                            pool.wait_ge(scattered[(q + 1) % QS], before * 16)
                        pool.sem_inc(pool_go, 1)
                        pool.indirect_dma_start(
                            out=m.rearrange("s (n a) -> (s n) a", a=1),
                            out_offset=bass.IndirectOffsetOnAxis(ap=lane_i[:, par, q:q + 1], axis=0),
                            in_=lane_v[:, par, q:q + 1], in_offset=None, compute_op=ALU.add).then_inc(scattered[q], 16)

            def whole(way):
                if way.hybrid:
                    wait_zeroed(pool, zeroed_counts)
                    scatter(0, counts, 0, True)
                    with pool.Fori(1, LAP // 2) as r:
                        scatter(0, counts, r, False)
                    wait_zeroed(pool, zeroed_weights)
                    with pool.Fori(0, LAP // 2) as r:
                        scatter(1, weights, r, False)
                stages(pool, way, gather)

            def gather(way, a, kind, layer):
                if kind == 0:
                    pool.wait_ge(v_tabs, 1)
                    pool.wait_ge(x_copied, 16)
                else:
                    pool.wait_ge(table_done, a * (GROUPS * 16))
                    pool.sem_inc(pool_go, 1)

                def lap(it, n):
                    for s in range(0, n, SUB):
                        ahead = AHEAD if way.hybrid else NQ
                        pool.wait_ge(pe_step, way.step(a) + it * RING + (s + SUB - ahead))
                        if s % NQ == 0:
                            pool.wait_ge(idx_staged, a * (way.chunks // NQ) + it * (RING // NQ) + (s // NQ + 1))
                        pool.sem_inc(pool_go, 1)
                        for c in range(s, s + SUB):
                            first = isinstance(it, int) and it * RING + c < NQ
                            if way.hybrid and not first:
                                pool.wait_ge(landed[c % NQ], (a * (way.chunks // NQ) + it * (RING // NQ) + c // NQ) * 16)
                                pool.sem_inc(pool_go, 1)
                            pool.indirect_dma_start(out=ring[:, c, :], out_offset=None, in_=table[:, :],
                                                    in_offset=bass.IndirectOffsetOnAxis(ap=stage[:, c:c + 1], axis=0)
                                                    ).then_inc(landed[c % NQ], 16)
                laps, rest = divmod(way.chunks, RING)
                if way.hybrid:
                    lap(0, RING)
                with pool.Fori(1 if way.hybrid else 0, laps) as it:
                    lap(it, RING)
                if rest:
                    lap(laps, rest)
            ways(pool, "pool", whole)

        @block.scalar
        def _(act):
            for i, n in enumerate(SQUARE):
                act.dma_start(wraw[:, i, :], A[n]).then_inc(in_w, 16)
            act.dma_start(wc[:, :], A["L1_gnn_W_conv"]).then_inc(in_w, 16)
            act.dma_start(wlin[:, :], A["L1_gnn_W_lin"]).then_inc(in_w, 16)
            act.dma_start(bc[:, :], A["L1_gnn_b_conv"].rearrange("(n a) -> n a", a=1)).then_inc(in_w, 16)
            act.dma_start(w2[:, 0, :], A["L2_gnn_W1"]).then_inc(in_w, 16)
            act.dma_start(w2[:, 1, :], A["L2_gnn_W2"]).then_inc(in_w, 16)
            act.dma_start(w3[:, :, :], A["L3_gnn_W"].rearrange("l k i o -> i (l k) o")).then_inc(in_w, 16)
            for i, n in enumerate(ROWS):
                act.dma_start(rows[:, i, :], A[n].partition_broadcast(P)).then_inc(in_w, 16)
            for i, n in enumerate(("bias", "gamma", "beta")):
                act.dma_start(rows3[:, i, :, :], A["L3_gnn_" + n].partition_broadcast(P)).then_inc(in_w, 16)

            act.wait_ge(v_nat, 4)
            zero(act, counts, zeroed_counts, act_go)

            def whole(way):
                if way.hybrid:
                    act.wait_ge(lanes_ready, 1)
                    halves = l_idx.bitcast(mybir.dt.uint16).rearrange("p (q r b) -> p r q b", r=LAP, b=2)
                    ones_v = l_one.rearrange("p (q r) -> p r q", r=LAP)
                    wgt_v = l_wgt.rearrange("p (q r) -> p r q", r=LAP)

                    def stage_round(which, r, par, first):
                        if not first:
                            for q in range(QS):
                                act.wait_ge(scattered[q], (which * LAP + par - 1) * 16 + r * 32)
                            act.sem_inc(act_go, 1)
                        this = bass.ds(r * 2 + par, 1)
                        act.activation(lane_i[:, par:par + 1, :].bitcast(mybir.dt.uint16).rearrange(
                            "p a (q b) -> p a q b", b=2), halves[:, this, :, :], ACT.Copy)
                        act.activation(lane_v[:, par:par + 1, :], (wgt_v if which else ones_v)[:, this, :],
                                       ACT.Copy).then_inc(lane_staged, 1)
                    stage_round(0, 0, 0, True)
                    stage_round(0, 0, 1, True)
                    for which in range(2):
                        with act.Fori(1 - which, LAP // 2) as r:
                            stage_round(which, r, 0, False)
                            stage_round(which, r, 1, False)
                act.wait_ge(v_steps, 2)
                act.activation(dtmp[:, :, :], dtmp[:, :, :], ACT.Sqrt).then_inc(a_deg, 1)
                stages(act, way, dense)
                with act.Fori(0, GROUPS) as g:
                    root(act, g + (3 + LAYERS) * GROUPS)

            def dense(way, a, kind, layer):
                if kind == 0:
                    act.wait_ge(v_tabs, 1)
                    wait_zeroed(act, zeroed_weights)

                def quarter(a, it, q):
                    act.wait_ge(pe_step, way.step(a) + it * RING + ((q + 1) * NQ - RING))
                    act.sem_inc(act_go, 1)
                    act.activation(stage[:, q * NQ:(q + 1) * NQ], src_idx[:, bass.ds(it * RING + q * NQ, NQ)],
                                   ACT.Copy).then_inc(idx_staged, 1)

                def first_lap(a):
                    for q in range(RING // NQ):
                        quarter(a, 0, q)
                if kind == 0:
                    first_lap(0)
                laps, rest = divmod(way.chunks, RING)
                with act.Fori(1, laps) as it:
                    for q in range(RING // NQ):
                        quarter(a, it, q)
                for q in range(rest // NQ):
                    quarter(a, laps, q)
                if way.hybrid:
                    act.wait_ge(swept, a * TILES + TILES)
                    act.sem_inc(act_go, 1)
                    for b in range(0, WIDE, 512):
                        last = act.activation(zflat[:, b:b + 512], pwide[:, b:b + 512], ACT.Copy)
                    last.then_inc(sweep_ready, 1)
                n = 2 * GT if uses_h(kind) else GT
                scale = scale_of(kind)

                def scaled(g):
                    for j in range(GT):
                        ins = act.activation(zin[:, j, :], acc[:, bass.ds(g * GT + j, 1), :], ACT.Copy,
                                             scale=scale[:, bass.ds(g * GT + j, 1)])
                    if uses_h(kind):
                        ins = act.activation(zin[:, GT:2 * GT, :], (xres if kind == 0 else hcur)[:, bass.ds(g * GT, GT), :],
                                             ACT.Copy)
                    ins.then_inc(z_ready, 1)

                def transposed(g):
                    act.wait_ge(zt_ps, a * GROUPS + g + 1)
                    act.sem_inc(act_go, 1)
                    for lo in range(0, n, 4):
                        hi = min(lo + 4, n)
                        last = act.activation(zT[:, lo:hi, :].rearrange("p t n -> p (t n)"),
                                              pT[:, lo * P:hi * P], ACT.Copy)
                    last.then_inc(zt_ready, 1)

                def hidden(g):
                    if kind == 2:
                        act.wait_ge(h64_ps, g + 1)
                        act.sem_inc(act_go, 1)
                        for lo, hi in ((0, 4), (4, 7)):
                            last = act.activation(zT[0:D1, GT + lo:GT + hi, :].rearrange("p t n -> p (t n)"),
                                                  pT[0:D1, lo * P:hi * P], ACT.Relu, bias=bc[:, :])
                        last.then_inc(h64_ready, 1)

                def norm(g):
                    first = {1: 0, 2: 1, 4: 2}.get(kind)
                    if first is not None:
                        root(act, first * GROUPS + g)
                    if kind == "hop3":
                        root(act, (layer + 3) * GROUPS + g)
                act.wait_ge(acc_final, a + 1)
                act.sem_inc(act_go, 1)
                first_lap(a + 1)
                scaled(0)
                transposed(0)
                scaled(1)
                hidden(0)
                with act.Fori(0, GROUPS - 2) as g:
                    transposed(g + 1)
                    norm(g)
                    scaled(g + 2)
                    hidden(g + 1)
                transposed(GROUPS - 1)
                norm(GROUPS - 2)
                hidden(GROUPS - 1)
                norm(GROUPS - 1)

            def root(act, n):
                act.wait_ge(var_ready, n + 1)
                act.sem_inc(act_go, 1)
                act.activation(sd[:, :], sd[:, :], ACT.Sqrt).then_inc(sd_ready, 1)
            ways(act, "act", whole)

        @block.tensor
        def _(pe):
            pe.wait_ge(g_const, 6)
            pe.wait_ge(p_walk, 1)
            for half in range(2):
                for k in range(CG):
                    pe.matmul(pT[:, half * 512:half * 512 + STEPS // 2], ones[:, :],
                              ge[:, k, half * (STEPS // 2):(half + 1) * (STEPS // 2)], start=(k == 0), stop=(k == CG - 1))
            for s in range(CG):
                n = min(P, STEPS - s * P)
                for k in range(CG):
                    last = pe.matmul(pT[0:n, 1024 + s:1025 + s], ge[:, k, s * P:s * P + n], ones[:, 0:1],
                                     start=(k == 0), stop=(k == CG - 1))
            last.then_inc(p_tabs, 1)
            pe.wait_ge(v_nat, 6)
            for k in range(CG):
                last = pe.transpose(pO[:, k * P:(k + 1) * P], snat[:, k, :], ident[:, :])
            last.then_inc(p_tabs, 1)
            pe.wait_ge(in_w, 16 * (10 + len(ROWS) + 3))
            for i in range(4):
                last = pe.transpose(pstep[0][:, i * P:(i + 1) * P], wraw[:, i, :], ident[:, :])
            last.then_inc(p_tabs, 1)
            pe.wait_ge(v_same, 1)
            pe.matmul(pstep[1][0:1, 0:1], same[:, :], ones[:, 0:1], start=True, stop=True).then_inc(p_flag, 1)
            pe.wait_ge(v_walk, 2)
            for k in range(CG):
                last = pe.transpose(pT[:, k * P:(k + 1) * P], dstep[:, k, :], ident[:, :])
            last.then_inc(p_tabs, 1)
            for k in range(CG):
                last = pe.transpose(pT[:, 1024 + k * P:1024 + (k + 1) * P], wstep[:, k, :], ident[:, :])
            last.then_inc(p_tabs, 1)
            pe.sem_inc(pe_step, STEP0)
            slots = [pe.alloc_register(f"pe_slot{j}") for j in range(BODY)]
            pe.wait_ge(v_tabs, 1)
            with pe.Fori(0, STEPS // BODY) as it:
                for j in range(BODY):
                    if j % BATCH == 0:
                        pe.wait_ge(hot_ready, it * (BODY // BATCH) + (j // BATCH + 1))
                        pe.sem_inc(pe_go, 1)
                        pe.wait_ge(acc_done, it * BODY + (ACC0 + j - (BATCH - 1)))
                        pe.sem_inc(pe_go, 1)
                    o = pstep[j // BATCH % 2][:, j % BATCH * 2:j % BATCH * 2 + 2]
                    pe.matmul(o[:, 0:1], hot[:, j, :], ones[:, 0:1], start=True, stop=True)
                    pe.matmul(o[:, 1:2], hot[:, j, :], wgt[:, bass.ds(it * BODY + j, 1)], start=True, stop=True
                              ).then_inc(pe_step, 1)

            def step(way, a, it, j, gathers, lag):
                if j % BATCH == 0:
                    pe.wait_ge(hot_ready, way.built(a) + it * (BODY // BATCH) + (j // BATCH + 1))
                    pe.wait_ge(acc_done, way.added(a) + it * BODY + (j - (BATCH - 1)))
                if gathers and not (isinstance(it, int) and it * BODY + j - lag >= C0):
                    pe.wait_ge(landed[(j - lag) % NQ], (a * (way.chunks // NQ) + it + (j - lag) // NQ + 1) * 16)
                pe.sem_inc(pe_go, 1)
                slot = pe.snap(slots[j], min_val=0, max_val=RING - 1)
                pe.matmul(pstep[j // BATCH % 2][:, j % BATCH * D:(j % BATCH + 1) * D], hot[:, j, :],
                          ring[:, bass.ds(slot, 1), :], start=True, stop=True).then_inc(pe_step, 1)

            def load_slots(it):
                for q in range(0, BODY, 4):
                    pe.load(slots[q:q + 4], slot_row[0:1, bass.ds(it * (BODY) + q, 4)])

            def walk(way, a, gathers, lo, hi, lag=0):
                with pe.Fori(lo, hi) as it:
                    load_slots(it)
                    for j in range(BODY):
                        step(way, a, it, j, gathers, lag)

            def both(way, a, it, last):
                load_slots(it)
                done = 0
                for m in range(12):
                    b = m % 6
                    if b == 0:
                        slot = 1 - m // 6
                        times = a * SWEEP + it + 1 if slot else a * (SWEEP + 1) + it + 2
                        pe.wait_ge(arrived[slot], times * 32)
                        pe.sem_inc(pe_go, 1)
                    mm = pe.matmul(pwide[:, b * 512:(b + 1) * 512], hrow[:, slot, :],
                                   matrix[:, slot, b * 512:(b + 1) * 512], start=False, stop=last and m >= 6)
                    if b == 5:
                        mm.then_inc(swept, 1)
                    while done < (m + 1) * 16 // 12:
                        step(way, a, it, done, True, 0)
                        done += 1

            def dense(way, a, kind, layer):
                if way.hybrid:
                    pe.wait_ge(post_done, a * GROUPS + 1)
                    pe.wait_ge(arrived[0], (a * (SWEEP + 1) + 1) * 32)
                    pe.sem_inc(pe_go, 1)
                    for b in range(6):
                        mm = pe.matmul(pwide[:, b * 512:(b + 1) * 512], hrow[:, 0, :],
                                       matrix[:, 0, b * 512:(b + 1) * 512], start=True, stop=False)
                    mm.then_inc(swept, 1)
                    with pe.Fori(0, SWEEP - 1) as it:
                        both(way, a, it, False)
                    both(way, a, SWEEP - 1, True)
                    walk(way, a, True, LAGS[0][0], LAGS[1][0], LAGS[0][1])
                    pe.wait_ge(sweep_ready, a + 1)
                    pe.sem_inc(pe_go, 1)
                    for j in range(TILES - T0):
                        mm = pe.transpose(pwide[:, j * P:(j + 1) * P], zflat[:, j * P:(j + 1) * P], ident[:, :])
                    mm.then_inc(merge_ps, 1)
                    walk(way, a, True, LAGS[1][0], WALK // BODY - 1, LAGS[1][1])
                    load_slots(WALK // BODY - 1)
                    for j in range(BODY):
                        step(way, a, WALK // BODY - 1, j, True, LAGS[1][1])
                else:
                    walk(way, a, True, 0, CHUNKS // NQ)
                    walk(way, a, False, CHUNKS // NQ, STEPS // NQ)
                n = 2 * GT if uses_h(kind) else GT
                with pe.Fori(0, GROUPS) as g:
                    pe.wait_ge(z_ready, a * GROUPS + g + 1)
                    pe.sem_inc(pe_go, 1)
                    for j in range(n):
                        last = pe.transpose(pT[:, j * P:(j + 1) * P], zin[:, j, :], ident[:, :])
                    last.then_inc(zt_ps, 1)
                    pe.wait_ge(zt_ready, a * GROUPS + g + 1)
                    pe.wait_ge(post_done, a * GROUPS + g + 1)
                    pe.sem_inc(pe_go, 1)
                    if kind == 2:
                        zf = zT[:, 0:GT, :].rearrange("p t n -> p (t n)")
                        for lo, hi in ((0, 512), (512, GT * P)):
                            last = pe.matmul(pT[0:D1, lo:hi], wc[:, :], zf[:, lo:hi], start=True, stop=True)
                        last.then_inc(h64_ps, 1)
                        pe.wait_ge(h64_ready, g + 1)
                        pe.sem_inc(pe_go, 1)
                    for j in range(GT):
                        o = pO[:, j * P:(j + 1) * P]
                        z, h = zT[:, j, :], zT[:, GT + j, :]
                        if kind in (0, 1):
                            last = pe.matmul(o, z, w0[:, 2 * kind, :], start=True, stop=False)
                            last = pe.matmul(o, h, w0[:, 2 * kind + 1, :], start=False, stop=True)
                        elif kind == 2:
                            last = pe.matmul(o, zT[0:D1, GT + j, :], wlin[:, :], start=True, stop=True)
                        elif kind in (3, 4):
                            last = pe.matmul(o, z, w2[:, kind - 3, :], start=True, stop=True)
                        else:
                            k = int(kind[3])
                            if k == 1:
                                pe.matmul(o, h, w3[:, bass.ds(layer * (HOPS + 1), 1), :], start=True, stop=False)
                            last = pe.matmul(o, z, w3[:, bass.ds(layer * (HOPS + 1) + k, 1), :],
                                             start=(k != 1), stop=True)
                    last.then_inc(o_ps, 1)
            ways(pe, "pe", lambda way: stages(pe, way, dense))

        @block.vector
        def _(dve):
            V = nc.vector
            count = [0]

            def link(ins):
                count[0] += 1
                ins.then_inc(v_chain, 1)
                dve.wait_ge(v_chain, count[0])

            V.memset(xres[:, TILES - 1, :], 0.0)
            V.memset(dnat_i, PAD_DST).then_inc(v_nat, 1)
            V.memset(snat_i, 0).then_inc(v_nat, 1)
            V.memset(wnat, 0.0).then_inc(v_nat, 1)
            V.memset(zflat, 0.0).then_inc(v_nat, 1)
            V.memset(chunk_idx[:, :], 0)
            V.memset(zero_col[:, :, :], 0.0)
            dve.sem_inc(post_done, 1)
            dve.sem_inc(tb_free, 1)
            dve.sem_inc(acc_done, ACC0)
            link(V.memset(chunk_col[:, :], 1.0))
            dve.wait_ge(in_edges, 144)
            V.tensor_copy(dnat, dnat_i).then_inc(v_nat, 1)
            V.tensor_copy(snat, snat_i).then_inc(v_nat, 1)
            dve.wait_ge(g_const, 6)
            V.tensor_copy(iota[:, :], iota_i[:, :])
            V.tensor_copy(step_f, step_i)
            link(V.tensor_copy(number[:, :], ci[:, :]))
            link(V.tensor_single_scalar(ci[:, :], dnat_i[:, :, 0], 7, ALU.arith_shift_right))
            link(V.tensor_copy(base_col[:, :], ci[:, :]))
            link(V.memset(base_col[0:1, 0:1], 0.0))
            link(V.tensor_scalar(base_col[:, :], base_col[:, :], float(TILES - 1), None, ALU.min))
            link(V.tensor_tensor(cf[:, :], number[:, :], base_col[:, :], ALU.add))
            for k in range(CG):
                last = V.tensor_scalar(ge[:, k, :], step_f, cf[:, k:k + 1], None, ALU.is_ge)
            last.then_inc(p_walk, 1)
            dve.wait_ge(p_tabs, 1)
            half = STEPS // 2
            for s in range(2):
                V.tensor_scalar(chunk_f[:, s * half:(s + 1) * half], pT[0:1, s * 512:s * 512 + half], -1.0, None, ALU.add)
            V.tensor_copy(chunk_col[:, 0:CG - 1], pT[:, 1024:1024 + CG - 1])
            tail = STEPS - (CG - 1) * P
            link(V.tensor_copy(chunk_col[0:tail, CG - 1:CG], pT[0:tail, 1024 + CG - 1:1024 + CG]))
            link(V.tensor_scalar(chunk_col[:, :], chunk_col[:, :], -1.0, None, ALU.add))
            V.tensor_copy(chunk_idx[:, :], chunk_col[:, :]).then_inc(v_walk, 1)
            link(V.tensor_tensor(tile_f, step_f[0:1, :], chunk_f, ALU.subtract))
            V.tensor_copy(tile_row[:, 0:STEPS], tile_f)
            link(V.tensor_copy(chunk_i, chunk_f))
            V.tensor_single_scalar(slot_row[:, 0:STEPS], chunk_i, RING - 1, ALU.bitwise_and)
            h = min(half, WALK)
            V.tensor_scalar(tail_mask[:, 0:h - C0], pT[:, C0:h], C0 + 0.5, 1e6, ALU.is_gt, ALU.mult)
            link(V.tensor_scalar(tail_mask[:, h - C0:WALK - C0], pT[:, 512:512 + WALK - h], C0 + 0.5, 1e6, ALU.is_gt, ALU.mult))
            dve.wait_ge(lanes_in, 80)
            link(V.tensor_scalar(l_one, l_dst, float(N), None, ALU.is_lt))
            link(V.tensor_tensor(l_dst2, l_dst, l_dst2, ALU.is_equal))
            link(V.tensor_tensor(l_dst2, l_dst2, l_one, ALU.mult))
            V.reduce_sum(same[:, :], l_dst2, axis=mybir.AxisListType.X).then_inc(v_same, 1)
            dve.wait_ge(v_same, 1)
            link(V.tensor_scalar(l_dst, l_dst, float(-T0 * P), None, ALU.add))
            link(V.tensor_tensor(l_dst, l_dst, step_f[:, 0:LANE], ALU.subtract))
            link(V.tensor_tensor(l_dst, l_dst, l_one, ALU.mult))
            link(V.tensor_tensor(l_dst, l_dst, step_f[:, 0:LANE], ALU.add))
            link(V.tensor_scalar(l_src, l_src, float(-PAD_SRC), None, ALU.add))
            link(V.tensor_tensor(l_src, l_src, l_one, ALU.mult))
            link(V.tensor_scalar(l_src, l_src, float(PAD_SRC), float(WIDE), ALU.add, ALU.mult))
            link(V.tensor_copy(l_ci, l_dst))
            link(V.tensor_copy(l_si, l_src))
            link(V.tensor_tensor(l_idx, l_ci, l_si, ALU.add))
            dve.sem_inc(lanes_ready, 1)
            dve.wait_ge(p_flag, 1)
            link(V.tensor_copy(flag[:, 0:1], first_dst[:, :]))
            link(V.tensor_scalar(flag[:, 1:2], flag[:, 0:1], float(T0 * P), None, ALU.is_ge))
            link(V.tensor_scalar(flag[:, 2:3], flag[:, 0:1], float((TEND + 1) * P), None, ALU.is_lt))
            link(V.tensor_scalar(flag[:, 3:4], pstep[1][0:1, 0:1], 0.5, None, ALU.is_lt))
            link(V.tensor_tensor(flag[:, 1:2], flag[:, 1:2], flag[:, 2:3], ALU.mult))
            link(V.tensor_tensor(flag[:, 1:2], flag[:, 1:2], flag[:, 3:4], ALU.mult))
            for body, lag in LAGS:
                link(V.tensor_scalar(flag[:, 2:3], tile_f[:, body * BODY:body * BODY + 1], float(lag), None, ALU.is_ge))
                link(V.tensor_tensor(flag[:, 1:2], flag[:, 1:2], flag[:, 2:3], ALU.mult))
            link(V.memset(flag_i[:, :], 0))
            link(V.tensor_copy(flag_i[:, 0:1], flag[:, 1:2]))
            dve.sem_inc(v_flag, 1)
            link(V.tensor_tensor(base_col[:, :], number[:, :], chunk_col[:, :], ALU.subtract))
            link(V.tensor_scalar(base_col[:, :], base_col[:, :], float(P), None, ALU.mult))
            dve.wait_ge(walk_dma, 16 * 2 * CG)
            for k in range(CG):
                last = V.tensor_scalar(dstep[:, k, :], dstep[:, k, :], base_col[:, k:k + 1], None, ALU.subtract)
            last.then_inc(v_walk, 1)
            dve.wait_ge(p_tabs, 2)
            V.tensor_copy(src_idx[:, :], pO[:, 0:CG * P])
            dve.wait_ge(p_tabs, 3)
            V.tensor_copy(w0[:, :, :].rearrange("p w d -> p (w d)"), pstep[0][:, :])
            dve.wait_ge(p_tabs, 5)
            V.tensor_copy(dst_rel[:, :], pT[:, 0:CG * P])
            link(V.tensor_copy(wgt[:, :], pT[:, 1024:1024 + CG * P]))
            dve.wait_ge(in_x, 32)
            dve.sem_inc(v_tabs, 1)
            tiles = [dve.alloc_register(f"dve_tile{j}") for j in range(SUB)]

            def build(it, j, weighted):
                i = it * BODY + j
                if weighted:
                    return V.tensor_scalar(hot[:, j % BODY, :], iota[:, :], dst_rel[:, bass.ds(i, 1)],
                                           wgt[:, bass.ds(i, 1)], ALU.is_equal, ALU.mult)
                return V.tensor_scalar(hot[:, j % BODY, :], iota[:, :], dst_rel[:, bass.ds(i, 1)], None, ALU.is_equal)

            def walk_start(weighted):
                for j in range(2 * BATCH):
                    ins = build(0, j, weighted)
                    if j % BATCH == BATCH - 1:
                        ins.then_inc(hot_ready, 1)

            def walk(stepped, added, lo, hi, weighted, to_all, width):
                with dve.Fori(lo, hi) as it:
                    for q in range(0, BODY, 4):
                        dve.load(tiles[q % 8:q % 8 + 4], tile_row[0:1, bass.ds(it * BODY + q, 4)])
                        for j in range(q, q + BATCH):
                            ins = build(it, j + 2 * BATCH, weighted)
                            if j % BATCH == BATCH - 1:
                                ins.then_inc(hot_ready, 1)
                            tile = dve.snap(tiles[j % 8], min_val=0, max_val=TILES - 1)
                            if j == q:
                                dve.wait_ge(pe_step, stepped + it * BODY + (j + BATCH))
                            dve.wait_ge(acc_done, added + it * BODY + (j + 1))
                            dve.sem_inc(dve_go, 1)
                            to = to_all[:, bass.ds(tile, 1), :]
                            c = j % BATCH * width
                            V.tensor_tensor(to, to, pstep[j // BATCH % 2][:, c:c + width].rearrange("p (a d) -> p a d", a=1),
                                            ALU.add).then_inc(acc_done, 1)
                dve.wait_ge(acc_done, added + (hi * BODY + 1))
                dve.sem_inc(dve_go, 1)

            V.memset(degs[:, :, :], 0.0).then_inc(acc_done, 1)
            walk_start(False)
            walk(STEP0, ACC0, 0, STEPS // BODY, False, degs, 2)

            def degrees():
                link(V.tensor_scalar(rcnt[:, :], degs[:, :, 0], 1.0, None, ALU.max))
                link(V.reciprocal(rcnt[:, :], rcnt[:, :]))
                link(V.tensor_scalar(degs[:, :, 0], degs[:, :, 0], 1.0, None, ALU.add))
                d2 = degs[:, :, :].rearrange("p t c -> p c t")
                link(V.tensor_scalar(dmask[:, :, :], d2, 0.0, None, ALU.is_gt))
                link(V.tensor_scalar(dinv[:, :, :], dmask[:, :, :], -1.0, 1.0, ALU.mult, ALU.add))
                link(V.tensor_tensor(dtmp[:, :, :], d2, dmask[:, :, :], ALU.mult))
                link(V.tensor_tensor(dtmp[:, :, :], dtmp[:, :, :], dinv[:, :, :], ALU.add))
                dve.sem_inc(v_steps, 2)
                dve.wait_ge(a_deg, 1)
                link(V.reciprocal(dinv[:, :, :], dtmp[:, :, :]))
                link(V.tensor_tensor(dinv[:, :, :], dinv[:, :, :], dmask[:, :, :], ALU.mult))

            def wide(col):
                return col.broadcast_to([P, GT, D])

            def column(x):
                return x.rearrange("p (t a) -> p t a", a=1)

            degrees()

            def whole(way):
                if way.hybrid:
                    link(V.tensor_tensor(dst_rel[:, C0:WALK], dst_rel[:, C0:WALK], tail_mask[:, :], ALU.add))
                stages(dve, way, dense)
                final()

            def dense(way, a, kind, layer):
                if kind in (0, "hop1"):
                    V.memset(acc[:, :, :], 0.0).then_inc(acc_done, 1)
                else:
                    dve.sem_inc(acc_done, 1)
                weighted = layer is not None
                walk_start(weighted)
                bodies = way.steps // BODY
                walk(way.step(a), way.added(a), 0, BIAS, weighted, acc, D)
                if kind in (1, 2, 4, "hop2"):
                    row = rows3[:, 0, bass.ds(layer, 1), :] if kind == "hop2" else rows[:, kind:kind + 1, :]
                    V.tensor_tensor(xres[:, :, :], xres[:, :, :], row.broadcast_to([P, TILES, D]), ALU.add)
                walk(way.step(a), way.added(a), BIAS, MERGE if way.hybrid else bodies, weighted, acc, D)
                if way.hybrid:
                    dve.wait_ge(merge_ps, a + 1)
                    dve.sem_inc(dve_go, 1)
                    V.tensor_tensor(acc[:, T0:TILES, :], acc[:, T0:TILES, :],
                                    pwide[:, :].rearrange("p (t d) -> p t d", d=D), ALU.add).then_inc(acc_merged, 1)
                    dve.wait_ge(acc_merged, a + 1)
                    dve.sem_inc(dve_go, 1)
                    walk(way.step(a), way.added(a), MERGE, bodies, weighted, acc, D)
                if kind == "hop1":
                    dve.wait_ge(kept, 16)
                scale = scale_of(kind)
                after = None if kind == 0 else dinv[:, 0, :] if kind in (1, 2, 3) else dinv[:, 1, :]

                def tile(g, j):
                    return bass.ds(g * GT + j, 1)

                def tiles_of(g):
                    return bass.ds(g * GT, GT)

                def passed_on(g):
                    for j in range(GT):
                        ins = V.tensor_scalar(ring[:, tile(g, j), :], acc[:, tile(g, j), :], scale[:, tile(g, j)],
                                              after[:, tile(g, j)], ALU.mult, ALU.mult)
                    ins.then_inc(tb_ready, 1)

                def finished(g):
                    G = a * GROUPS + g
                    links = [0]

                    def chained(ins):
                        links[0] += 1
                        ins.then_inc(v_group, 1)
                        dve.wait_ge(v_group, G * LINKS + links[0])
                        dve.sem_inc(dve_go, 1)
                    sl = tiles_of(g)
                    dve.wait_ge(o_ps, G + 1)
                    dve.sem_inc(dve_go, 1)
                    po = pO[:, 0:GT * P].rearrange("p (t d) -> p t d", t=GT)
                    if kind == "hop1":
                        V.tensor_tensor(outacc[:, sl, :], po, hcur[:, sl, :], ALU.add).then_inc(post_done, 1)
                    elif kind == "hop2":
                        V.tensor_tensor(outacc[:, sl, :], outacc[:, sl, :], po, ALU.add).then_inc(post_done, 1)
                    elif kind in (0, 3):
                        chained(V.tensor_tensor(t[:, :, :], po, rows[:, kind:kind + 1, :].broadcast_to([P, GT, D]), ALU.add))
                        dve.sem_inc(post_done, 1)
                        if kind == 0:
                            V.tensor_scalar(hcur[:, sl, :], t[:, :, :], 0.0, None, ALU.max).then_inc(tb_ready, 1)
                        else:
                            for j in range(GT):
                                ins = V.tensor_scalar(acc[:, tile(g, j), :], t[:, j, :], 0.0, after[:, tile(g, j)],
                                                      ALU.max, ALU.mult)
                            ins.then_inc(tb_ready, 1)
                    else:
                        chained(V.tensor_tensor(t[:, :, :], po, (outacc if kind == "hop3" else xres)[:, sl, :], ALU.add))
                        dve.sem_inc(post_done, 1)
                        first = {1: 0, 2: 1, 4: 2}.get(kind)
                        n = first * GROUPS + g if first is not None else (layer + 3) * GROUPS + g
                        if kind == "hop3":
                            moments(n, chained)
                            gamma, beta = (rows3[:, i, bass.ds(layer, 1), :] for i in (1, 2))
                            for j in range(GT):
                                ins = V.scalar_tensor_tensor(t[:, j, :], t[:, j, :], mv[:, j, 0:1], gamma, ALU.subtract, ALU.mult)
                            chained(ins)
                            for j in range(GT):
                                ins = V.scalar_tensor_tensor(t[:, j, :], t[:, j, :], rstd[:, j:j + 1], beta, ALU.mult, ALU.add)
                            chained(ins)
                            V.tensor_scalar(hcur[:, sl, :], t[:, :, :], 0.0, None, ALU.max)
                        else:
                            new = hcur if kind == 4 else xres
                            normalise(n, chained, lambda j: new[:, tile(g, j), :])
                        if kind in (1, 2):
                            for j in range(GT):
                                ins = V.tensor_scalar(acc[:, tile(g, j), :], new[:, tile(g, j), :],
                                                      after[:, tile(g, j)], None, ALU.mult)
                        else:
                            dve.wait_ge(tb_free, G + 1)
                            dve.sem_inc(dve_go, 1)
                            for j in range(GT):
                                if kind == "hop3":
                                    ins = V.tensor_scalar(tb[:, j, :], t[:, j, :], 0.0, after[:, tile(g, j)],
                                                          ALU.max, ALU.mult)
                                else:
                                    ins = V.tensor_scalar(tb[:, j, :], new[:, tile(g, j), :], after[:, tile(g, j)],
                                                          None, ALU.mult)
                        ins.then_inc(tb_ready, 1)
                    if kind not in ("hop1", "hop2"):
                        dve.wait_ge(tb_ready, G + 1)
                        dve.sem_inc(dve_go, 1)
                    if kind in (0, "hop1", "hop2"):
                        chained(V.tensor_copy(acc[:, sl, :], zero_col[:, :, :].broadcast_to([P, GT, D])))
                    dve.wait_ge(post_done, G + 2)
                    dve.sem_inc(dve_go, 1)
                    dve.sem_inc(v_group, LINKS - links[0])
                    assert links[0] < LINKS

                dve.sem_inc(acc_final, 1)
                if kind in ("hop1", "hop2"):
                    with dve.Fori(0, GROUPS) as g:
                        passed_on(g)
                    dve.wait_ge(tb_ready, (a + 1) * GROUPS)
                    dve.sem_inc(dve_go, 1)
                with dve.Fori(0, GROUPS) as g:
                    finished(g)

            def moments(n, chained):
                for j in range(GT):
                    ins = V.bn_stats(stats[:, j, :], t[:, j, :])
                chained(ins)
                for j in range(GT):
                    ins = V.bn_aggr(mv[:, j, :], stats[:, j, :])
                chained(ins)
                chained(V.tensor_scalar(sd[:, :], mv[:, :, 1], EPS, None, ALU.add))
                dve.sem_inc(var_ready, 1)
                dve.wait_ge(sd_ready, n + 1)
                dve.sem_inc(dve_go, 1)
                chained(V.reciprocal(rstd[:, :], sd[:, :]))

            def normalise(n, chained, to):
                moments(n, chained)
                for j in range(GT):
                    ins = V.tensor_scalar(to(j), t[:, j, :], mv[:, j, 0:1], rstd[:, j:j + 1], ALU.subtract, ALU.mult)
                chained(ins)

            def final():
                total = STAGES + LAYERS * HOPS
                for g in range(GROUPS):
                    G = g + total * GROUPS
                    start = [0]

                    def chained(ins):
                        start[0] += 1
                        ins.then_inc(v_group, 1)
                        dve.wait_ge(v_group, G * LINKS + start[0])
                    sl = slice(g * GT, (g + 1) * GT)
                    dve.wait_ge(back[g], 16)
                    chained(V.tensor_tensor(t[:, :, :], xres[:, sl, :], hcur[:, sl, :], ALU.add))
                    normalise(g + (3 + LAYERS) * GROUPS, chained, lambda j: acc[:, g * GT + j, :])
                    dve.sem_inc(tb_ready, 1)
                    dve.sem_inc(v_group, LINKS - start[0])

            ways(dve, "dve", whole)


_INS = ["x", "src", "dst", "edge_weight", "L0_gnn_W1l", "L0_gnn_b1l", "L0_gnn_W1r", "L0_gnn_W2l", "L0_gnn_b2l",
        "L0_gnn_W2r", "L1_gnn_W_conv", "L1_gnn_b_conv", "L1_gnn_W_lin", "L1_gnn_b_lin", "L2_gnn_W1", "L2_gnn_b1",
        "L2_gnn_W2", "L2_gnn_b2", "L3_gnn_W", "L3_gnn_bias", "L3_gnn_gamma", "L3_gnn_beta"]


def kernel(**inputs):
    import numpy as np
    import concourse.bacc as bacc
    from concourse.bass_utils import run_bass_kernel_spmd

    nc = bacc.Bacc("TRN2", target_bir_lowering=False, num_devices=1)
    arrays, A = {}, {}
    for name in _INS:
        a = np.ascontiguousarray(inputs[name])
        arrays[f"in_{name}"] = a
        A[name] = nc.dram_tensor(f"in_{name}", a.shape, mybir.dt.from_np(a.dtype), kind="ExternalInput").ap()
    out = nc.dram_tensor("out", (N, D), F32, kind="ExternalOutput").ap()
    program(nc, A, out)
    r = run_bass_kernel_spmd(nc, [arrays], core_ids=[0])
    return r.results[0]["out"]
```
